# Optimizing a Trainium2 kernel written in Bass

```python
import numpy as np
import jax
import jax.numpy as jnp

def _softmax(x, axis=-1):
    return jax.nn.softmax(x, axis=axis)

def _gelu(x):
    return jax.nn.gelu(x, approximate=True)

def _silu(x):
    return jax.nn.silu(x)

def _sigmoid(x):
    return jax.nn.sigmoid(x)

def _layernorm(x, axis=-1, eps=1e-05):
    m = jnp.mean(x, axis=axis, keepdims=True)
    v = jnp.var(x, axis=axis, keepdims=True)
    return (x - m) / jnp.sqrt(v + eps)

def _scatter_add(tgt, idx, src, axis=0):
    return tgt.at[idx].add(src)

def _segment_sum(src, seg, n):
    return jax.ops.segment_sum(src, seg, n)
kernel_name = 'mk_seq_postln_d1_jaxref_r8_3d4cdb'

def setup_inputs(seed: int=0):
    np.random.seed(seed)
    _w = jnp.asarray

    def _L0_attn_setup():
        import jax, jax.numpy as jnp
        import numpy as np
        BATCH, SEQ, HIDDEN = (2, 512, 512)
        HEADS, HEAD_DIM, BLOCK = (32, 128, 32)
        LAYER_IDX, N_LAYERS = (1, 32)
        EPS = 1e-05

        def _decays():
            base = 1.0 / 2.0 ** (8.0 / HEADS)
            exponent = jnp.arange(HEADS, dtype=jnp.float32) + 1.0
            factor = 1.0 - LAYER_IDX / (N_LAYERS - 1 + 1e-05) + 1e-05
            slope = (base ** exponent * factor)[:, None, None]
            r = jnp.arange(BLOCK, dtype=jnp.float32) + 1.0
            q_decay = jnp.exp(-slope * r[:, None])
            k_decay = jnp.exp(-slope * (BLOCK - r)[:, None])
            diff = r[:, None] - r[None, :]
            diag = slope[None] * diff[None, None]
            diag = jnp.where(diag >= 0, -diag, -jnp.inf)
            diag_decay = jnp.exp(diag)
            block_decay = jnp.exp(-slope * BLOCK)
            return (q_decay, k_decay, diag_decay, block_decay)
        key = jax.random.key(seed)
        ks = jax.random.split(key, 5)
        s = 0.02
        return {'hidden_states': jax.random.normal(ks[0], (BATCH, SEQ, HIDDEN), jnp.float32), 'qkv_w': jax.random.normal(ks[1], (3 * HEADS * HEAD_DIM, HIDDEN), jnp.float32) * s, 'out_w': jax.random.normal(ks[2], (HIDDEN, HEADS * HEAD_DIM), jnp.float32) * s, 'gate_w': jax.random.normal(ks[3], (HEADS * HEAD_DIM, HIDDEN), jnp.float32) * s, 'norm_w': jnp.ones((HEADS * HEAD_DIM,), jnp.float32)}
    _L0_attn_in = _L0_attn_setup()

    def _L0_ffn_setup():
        import jax, jax.numpy as jnp
        import numpy as np
        SCALING = 32.0 / 16.0
        key = jax.random.key(seed)
        ks = jax.random.split(key, 7)
        B, T, D, O, R, E = (4, 256, 512, 512, 16, 8)
        x = jax.random.normal(ks[0], (B, T, D), dtype=jnp.float32)
        base_W = jax.random.normal(ks[1], (O, D), dtype=jnp.float32) * D ** (-0.5)
        base_b = jax.random.normal(ks[2], (O,), dtype=jnp.float32) * 0.01
        router_W = jax.random.normal(ks[3], (2 * E - 1, D), dtype=jnp.float32) * D ** (-0.5)
        router_b = jax.random.normal(ks[4], (2 * E - 1,), dtype=jnp.float32) * 0.01
        A = jax.random.normal(ks[5], (E, R, D), dtype=jnp.float32) * D ** (-0.5)
        Bm = jax.random.normal(ks[6], (E, O, R), dtype=jnp.float32) * R ** (-0.5)
        assigned_idx = 0
        others = [i for i in range(E) if i != assigned_idx]
        expert_map = jnp.array([assigned_idx] * E + others, dtype=jnp.int32)
        return {'x': x, 'base_W': base_W, 'base_b': base_b, 'router_W': router_W, 'router_b': router_b, 'A': A, 'B': Bm, 'expert_map': expert_map}
    _L0_ffn_in = _L0_ffn_setup()
    _d = {'L0_attn_hidden_states': _L0_attn_in['hidden_states'], 'L0_attn_qkv_w': _L0_attn_in['qkv_w'], 'L0_attn_out_w': _L0_attn_in['out_w'], 'L0_attn_gate_w': _L0_attn_in['gate_w'], 'L0_attn_norm_w': _L0_attn_in['norm_w'], 'L0_ffn_base_W': _L0_ffn_in['base_W'], 'L0_ffn_base_b': _L0_ffn_in['base_b'], 'L0_ffn_router_W': _L0_ffn_in['router_W'], 'L0_ffn_router_b': _L0_ffn_in['router_b'], 'L0_ffn_A': _L0_ffn_in['A'], 'L0_ffn_B': _L0_ffn_in['B'], 'L0_ffn_expert_map': _L0_ffn_in['expert_map']}
    _x0 = _d['L0_attn_hidden_states']
    _d['L0_attn_hidden_states'] = jax.random.normal(jax.random.fold_in(jax.random.key(seed), 1), (4, 256, 512), dtype=_x0.dtype)
    del _x0
    return _d

def reference(L0_attn_hidden_states, L0_attn_qkv_w, L0_attn_out_w, L0_attn_gate_w, L0_attn_norm_w, L0_ffn_base_W, L0_ffn_base_b, L0_ffn_router_W, L0_ffn_router_b, L0_ffn_A, L0_ffn_B, L0_ffn_expert_map):

    def _L0_attn_ref(hidden_states, qkv_w, out_w, gate_w, norm_w):
        import jax, jax.numpy as jnp
        import numpy as np
        BATCH, SEQ, HIDDEN = (2, 512, 512)
        HEADS, HEAD_DIM, BLOCK = (32, 128, 32)
        LAYER_IDX, N_LAYERS = (1, 32)
        EPS = 1e-05

        def _decays():
            base = 1.0 / 2.0 ** (8.0 / HEADS)
            exponent = jnp.arange(HEADS, dtype=jnp.float32) + 1.0
            factor = 1.0 - LAYER_IDX / (N_LAYERS - 1 + 1e-05) + 1e-05
            slope = (base ** exponent * factor)[:, None, None]
            r = jnp.arange(BLOCK, dtype=jnp.float32) + 1.0
            q_decay = jnp.exp(-slope * r[:, None])
            k_decay = jnp.exp(-slope * (BLOCK - r)[:, None])
            diff = r[:, None] - r[None, :]
            diag = slope[None] * diff[None, None]
            diag = jnp.where(diag >= 0, -diag, -jnp.inf)
            diag_decay = jnp.exp(diag)
            block_decay = jnp.exp(-slope * BLOCK)
            return (q_decay, k_decay, diag_decay, block_decay)
        b, s, _ = hidden_states.shape
        h, d, bs = (HEADS, HEAD_DIM, BLOCK)
        nb = s // bs
        q_decay, k_decay, diag_decay, block_decay = _decays()
        qkv = jax.nn.silu(hidden_states @ qkv_w.T)
        qkv = qkv.reshape(b, s, h, 3, d)
        q = jnp.moveaxis(qkv[:, :, :, 0], 2, 1)
        k = jnp.moveaxis(qkv[:, :, :, 1], 2, 1)
        v = jnp.moveaxis(qkv[:, :, :, 2], 2, 1)

        def to_blocks(x):
            return jnp.moveaxis(x.reshape(b, h, nb, bs, d), 2, 0)
        qb, kb, vb = (to_blocks(q), to_blocks(k), to_blocks(v))

        def step(kv, blk):
            cq, ck, cv = blk
            scores = jnp.einsum('bhnd,bhmd->bhnm', cq, ck) * diag_decay
            intra = jnp.einsum('bhnm,bhmd->bhnd', scores, cv)
            inter = jnp.einsum('bhnd,bhde->bhne', cq * q_decay, kv)
            kv_next = kv * block_decay + jnp.einsum('bhnd,bhne->bhde', ck * k_decay, cv)
            return (kv_next, intra + inter)
        kv0 = jnp.zeros((b, h, d, d), hidden_states.dtype)
        _, out_blocks = jax.lax.scan(step, kv0, (qb, kb, vb))
        attn = jnp.moveaxis(out_blocks, 0, 2)
        attn = attn.reshape(b, h, s, d).transpose(0, 2, 1, 3).reshape(b, s, h * d)
        xf = attn.astype(jnp.float32)
        xf = xf * jax.lax.rsqrt(jnp.mean(xf * xf, axis=-1, keepdims=True) + EPS)
        normed = norm_w * xf.astype(attn.dtype)
        gate = jax.nn.sigmoid(hidden_states @ gate_w.T)
        return gate * normed @ out_w.T

    def _L0_ffn_ref(x, base_W, base_b, router_W, router_b, A, B, expert_map):
        import jax, jax.numpy as jnp
        import numpy as np
        SCALING = 32.0 / 16.0
        E = A.shape[0]
        base_out = jnp.einsum('btd,od->bto', x, base_W) + base_b
        logits = jnp.einsum('btd,nd->btn', x, router_W) + router_b
        probs = jax.nn.softmax(logits, axis=-1)
        topk_p, topk_i = jax.lax.top_k(probs, E)
        mapped = expert_map[topk_i]
        onehot = (mapped[..., None] == jnp.arange(E)).astype(x.dtype)
        w = jnp.einsum('btk,btke->bte', topk_p, onehot)
        h = jnp.einsum('btd,erd->bter', x, A)
        lora = jnp.einsum('bter,eor->bto', h * w[..., None], B) * SCALING
        return base_out + lora
    x = L0_attn_hidden_states
    x = _layernorm(x + _L0_attn_ref(x, L0_attn_qkv_w, L0_attn_out_w, L0_attn_gate_w, L0_attn_norm_w), axis=-1)
    x = _layernorm(x + _L0_ffn_ref(x, L0_ffn_base_W, L0_ffn_base_b, L0_ffn_router_W, L0_ffn_router_b, L0_ffn_A, L0_ffn_B, L0_ffn_expert_map), axis=-1)
    return x

_drawn_inputs = setup_inputs


def setup_inputs(seed=0):
    import zlib

    import numpy as np

    out = dict(_drawn_inputs(seed))
    spreads = {'L0_attn_norm_w': (1.0, 0.2)}
    factors = {'L0_ffn_base_b': 8.0, 'L0_ffn_router_b': 7.134}
    for name, (base, spread) in spreads.items():
        noise = np.random.default_rng([zlib.crc32(name.encode()), seed]).standard_normal(out[name].shape)
        drawn = base * np.exp(spread * noise) if base else spread * noise
        out[name] = jnp.asarray(drawn.astype(out[name].dtype))
    for name, factor in factors.items():
        out[name] = (out[name] * factor).astype(out[name].dtype)
    return out
```

```python
import numpy as np
import concourse.bass as bass
from concourse import mybir
from concourse.alu_op_type import AluOpType as ALU
from contextlib import ExitStack

FP32 = mybir.dt.float32
FP32R = mybir.dt.float32r
I32 = mybir.dt.int32
ACT = mybir.ActivationFunctionType
AX = mybir.AxisListType

P = 128
BATCH, SEQ, HID = 4, 256, 512
TOK = BATCH * SEQ
TT = TOK // P
HEADS, BLOCK = 32, 32
KT = HID // P
HG = 4
GROUPS = HEADS // HG
W = 512
SC = SEQ + P
NEXP, NROUTE, RANK = 8, 15, 16
SCALING = 2.0
EPS = 1e-5

CHUNKS = (["q", "v", "v", "v", "v", "k", "g"] + ["q", "o", "o", "o", "o", "k", "g"]
          + ["q", "k", "g"] + ["q", "k", "g"])
NCH = len(CHUNKS)
QCH = [0, 7, 14, 17]
KCH = [5, 12, 15, 18]
GCH = [6, 13, 16, 19]
VCH, OCH = 1, 8
AHEAD = 10
RAW = 5
XCH = 2 * KT
TAIL_OCH, BASECH, ACH, BCH = 0, 4, 8, 9
CONSTS = 8
NSTREAM = XCH + GROUPS * NCH + AHEAD

PROJ = ["q"] * 2 + ["v"] * TT + ["k"] * 2 + ["g"] * 2 + (["q"] * 2 + ["k"] * 2 + ["g"] * 2) * 3
NPROJ = len(PROJ)
NSILU = sum(j != "g" for j in PROJ)
NGATE = NPROJ - NSILU
QJOB, KJOB, GJOB, VJOB = [0, 14, 20, 26], [10, 16, 22, 28], [12, 18, 24, 30], 2


def silu_no(i):
    return sum(j != "g" for j in PROJ[:i])


def gate_no(i):
    return sum(j == "g" for j in PROJ[:i])


def build(nc, stream, x, decay, norm_w, base_b, router_w, router_b, expert_map, ident_in, ones_in, order_in, out):
    ctx = ExitStack()
    with ctx:
        def sb(name, shape, dt=FP32):
            return ctx.enter_context(nc.sbuf_tensor(name, shape, dt))

        def sem(name):
            return ctx.enter_context(nc.semaphore(name))

        raw = sb("raw", [P, RAW, W])
        wh = sb("wh", [P, AHEAD, W], FP32R)
        wl = sb("wl", [P, AHEAD, W], FP32R)
        xh = sb("xh", [P, KT, TOK], FP32R)
        xl = sb("xl", [P, KT, TOK], FP32R)
        qh = sb("qh", [P, TOK], FP32R)
        ql = sb("ql", [P, TOK], FP32R)
        kh = sb("kh", [P, TOK], FP32R)
        kl = sb("kl", [P, TOK], FP32R)
        vh = sb("vh", [P, TT, W], FP32R)
        vl = sb("vl", [P, TT, W], FP32R)
        sh = sb("sh", [P, BATCH, SC], FP32R)
        sl = sb("sl", [P, BATCH, SC], FP32R)
        yh = sb("yh", [P, HG, TOK], FP32R)
        yl = sb("yl", [P, HG, TOK], FP32R)
        sig = sb("sig", [P, 2, W])
        gate = sb("gate", [P, 2, W])
        sfull = sb("sfull", [P, 2, SC])
        sq = sb("sq", [P, 2, W])
        sqacc = sb("sqacc", [P, 2, W])
        acc = sb("acc", [P, TT, HID])
        dec = sb("dec", [P, 2, SC])
        nw = sb("nw", [P, HEADS])
        ident = sb("ident", [P, P])
        ones = sb("ones", [P, 2])
        rw = sb("rw", [P, KT, RANK])
        rh = sb("rh", [P, KT, RANK], FP32R)
        rl = sb("rl", [P, KT, RANK], FP32R)
        bb = sb("bb", [P, HID])
        rb = sb("rb", [P, NROUTE])
        emap = sb("emap", [P, NROUTE], I32)
        order = sb("order", [P, 2, NROUTE, NROUTE])
        route = sb("route", [P, NEXP, NROUTE])
        rms = sb("rms", [P, TT])
        stat = sb("stat", [P, TT, 6])
        mv = sb("mv", [P, TT, 2])
        rstd = sb("rstd", [P, TT])
        rs_v = sb("rs_v", [P, TT])
        rs_t = sb("rs_t", [P, TT])
        prob = sb("prob", [P, HG, NROUTE])
        red = sb("red", [P, HG])
        def as_cmp(buf):
            flat = buf[:, :, :].rearrange("p a n -> p (a n)")[:, 0:HG * NROUTE * NROUTE]
            return flat.rearrange("p (t i j) -> p t i j", t=HG, i=NROUTE)

        cmp_a, cmp_b = as_cmp(sig), as_cmp(gate)
        rank = sb("rank", [P, HG, NROUTE])
        wexp = sb("wexp", [P, HG, NEXP, NROUTE])
        wsum = sb("wsum", [P, HG, NEXP])
        hw = sb("hw", [P, HG, P])
        ps = ctx.enter_context(nc.psum_tensor("ps", [P, 8, W], FP32))
        PROJ_B, S_B, AO_B = 0, 4, 6

        raw_in = [sem(f"raw_in{i}") for i in range(RAW)]
        dec_in = [sem(f"dec_in{i}") for i in range(2)]
        const_in = sem("const_in")
        stored = [sem(f"stored{t}") for t in range(TT)]
        split_hi, split_lo = sem("split_hi"), sem("split_lo")
        router_hi, router_lo = sem("router_hi"), sem("router_lo")
        proj_done, sig_done, silu_full = sem("proj_done"), sem("sig_done"), sem("silu_full")
        silu_hi, silu_lo, gate_done = sem("silu_hi"), sem("silu_lo"), sem("gate_done")
        s_done, s_full, s_hi, s_lo = sem("s_done"), sem("s_full"), sem("s_hi"), sem("s_lo")
        att_done, sq_done, sq_added = sem("att_done"), sem("sq_done"), sem("sq_added")
        y_full, y_hi, y_lo = sem("y_full"), sem("y_hi"), sem("y_lo")
        o_done, o_added = sem("o_done"), sem("o_added")
        ss_done, x1_done, ln1_done, bias_added = sem("ss_done"), sem("x1_done"), sem("ln1_done"), sem("bias_added")
        tr_done, tr_hi, tr_lo = sem("tr_done"), sem("tr_hi"), sem("tr_lo")
        hl_done, shifted, exp_done, hw_done = sem("hl_done"), sem("shifted"), sem("exp_done"), sem("hw_done")
        ht_done, ht_hi, ht_lo = sem("ht_done"), sem("ht_hi"), sem("ht_lo")
        ffn_done, ffn_read, out_ready = sem("ffn_done"), sem("ffn_read"), sem("out_ready")
        dve_step = sem("dve_step")

        block = ctx.enter_context(nc.Block())

        def half(i):
            return slice(i * W, i * W + W)

        def tile(t):
            return slice(t * P, t * P + P)

        def f32(ap):
            return ap.bitcast(FP32)

        @block.sync
        def _(sp):
            def load(m, slot, pos):
                sp.dma_start(raw[:, slot, :], stream[m]).then_inc(raw_in[slot], 16)

            for m in range(RAW):
                load(m, m, m)
            for dst, src in ((nw[:, :], norm_w), (ident[:, :], ident_in), (ones[:, :], ones_in),
                             (bb[:, :], base_b.partition_broadcast(P)), (rb[:, :], router_b.partition_broadcast(P)),
                             (emap[:, :], expert_map.partition_broadcast(P)), (rw[:, :, :], router_w),
                             (order[:, :, :, :], order_in.partition_broadcast(P))):
                sp.dma_start(dst, src).then_inc(const_in, 16)
            for m in range(RAW, XCH + AHEAD):
                sp.wait_ge(split_lo, m - RAW + 1)
                sp.dma_start(raw[:, m % RAW, :], stream[m]).then_inc(raw_in[m % RAW], 16)
            with sp.Fori(0, GROUPS) as g:
                for j in range(NCH):
                    m0 = XCH + AHEAD + j
                    sp.wait_ge(split_lo, g * NCH + (m0 - RAW + 1))
                    src = stream[bass.ds(g * NCH + m0, 1), :, :].rearrange("a p n -> p (a n)")
                    sp.dma_start(raw[:, m0 % RAW, :], src).then_inc(raw_in[m0 % RAW], 16)
            for t in range(TT):
                m = NSTREAM + t
                if t < RAW:
                    sp.wait_ge(split_lo, m - RAW + 1)
                else:
                    sp.wait_ge(x1_done, t - RAW + 1)
                sp.dma_start(raw[:, m % RAW, :], x[tile(t), :]).then_inc(raw_in[m % RAW], 16)
            for t in range(TT):
                sp.wait_ge(out_ready, t + 1)
                sp.dma_start(out[tile(t), :], acc[:, t, :]).then_inc(stored[t], 16)
            for t in range(TT):
                sp.wait_ge(stored[t], 16)

        def arrived(eng, g, m0):
            eng.wait_ge(raw_in[m0 % RAW], g * (16 * NCH // RAW) + 16 * (m0 // RAW + 1))

        def split_dst(m, xs, ws):
            if m == KT:
                return ws[:, 0, :]
            if m > XCH:
                return ws[:, m - XCH, :]
            c = m if m < KT else m - 1
            return xs[:, c % KT, half(c // KT)]

        @block.scalar
        def _(act):
            def load_decay(h, slot):
                src = decay[bass.ds(h, 1), :, :].rearrange("a p n -> p (a n)")
                act.dma_start(dec[:, slot, :], src).then_inc(dec_in[slot], 16)

            def split_chunk(g, u):
                arrived(act, g, XCH + AHEAD + u)
                kind, s = CHUNKS[u], sum(c == "k" for c in CHUNKS[:u])
                if kind != "o":
                    last = {"q": lambda: QJOB[s] + 2, "v": lambda: VJOB + TT, "k": lambda: KJOB[s] + 2, "g": lambda: GJOB[s - 1] + 2}[kind]()
                    act.wait_ge(proj_done, g * NPROJ + last)
                elif not isinstance(g, int):
                    act.wait_ge(o_done, g * TT)
                nc.scalar.activation(wh[:, u % AHEAD, :], raw[:, (XCH + AHEAD + u) % RAW, :], ACT.Copy)\
                    .then_inc(split_hi, 1)

            def front(g, i):
                n = silu_no(i)
                act.wait_ge(proj_done, g * NPROJ + (i + 1))
                if n >= 2 or not isinstance(g, int):
                    act.wait_ge(silu_lo, g * NSILU + (n - 1))
                nc.scalar.activation(sig[:, n % 2, :], ps[:, PROJ_B + i % 4, :], ACT.Sigmoid).then_inc(sig_done, 1)

            def back(g, i, dst):
                n = silu_no(i)
                act.wait_ge(silu_full, g * NSILU + (n + 1))
                nc.scalar.activation(dst, sig[:, n % 2, :], ACT.Copy).then_inc(silu_hi, 1)

            def gate_half(g, s, e):
                i = GJOB[s] + e
                act.wait_ge(proj_done, g * NPROJ + (i + 1))
                if s > 0 or not isinstance(g, int):
                    act.wait_ge(y_lo, g * (2 * HG) + (2 * (s - 1) + e + 1))
                nc.scalar.activation(gate[:, e, :], ps[:, PROJ_B + i % 4, :], ACT.Sigmoid).then_inc(gate_done, 1)

            def scores(g, s):
                for b in range(BATCH):
                    act.wait_ge(s_full, g * (HG * BATCH) + (s * BATCH + b + 1))
                    nc.scalar.activation(sh[:, b, :], sfull[:, b % 2, :], ACT.Copy).then_inc(s_hi, 1)

            def attention(g, s):
                r = (s - 1) % HG
                for e in range(2):
                    a = 2 * (s - 1) + e
                    act.wait_ge(att_done, g * (2 * HG) + (a + 1))
                    if a >= 2 or not isinstance(g, int) or g > 0:
                        act.wait_ge(sq_added, g * (2 * HG) + (a + 1))
                    nc.scalar.activation(sq[:, e, :], ps[:, AO_B + e, :], ACT.Square).then_inc(sq_done, 1)
                for e in range(2):
                    act.wait_ge(y_full, g * (2 * HG) + (2 * (s - 1) + e + 1))
                    nc.scalar.activation(yh[:, r, half(e)], gate[:, e, :], ACT.Copy).then_inc(y_hi, 1)

            def group(g, first):
                for s in range(HG):
                    q, k = QJOB[s], KJOB[s]
                    front(g, q)
                    front(g, q + 1)
                    back(g, q, qh[:, half(0)])
                    split_chunk(g, QCH[s])
                    back(g, q + 1, qh[:, half(1)])
                    if s > 0 or not first:
                        attention(g, s)
                    if s == 0:
                        for t in range(TT):
                            front(g, VJOB + t)
                            if t:
                                back(g, VJOB + t - 1, vh[:, t - 1, :])
                        front(g, k)
                        back(g, VJOB + TT - 1, vh[:, TT - 1, :])
                    else:
                        front(g, k)
                    c = {0: VCH, 1: OCH}.get(s)
                    if c is not None:
                        split_chunk(g, c)
                    front(g, k + 1)
                    back(g, k, kh[:, half(0)])
                    back(g, k + 1, kh[:, half(1)])
                    if c is not None:
                        split_chunk(g, c + 1)
                    gate_half(g, s, 0)
                    if c is not None:
                        split_chunk(g, c + 2)
                    gate_half(g, s, 1)
                    if c is not None:
                        split_chunk(g, c + 3)
                    scores(g, s)
                    load_decay(g * HG + (s + 2), s % 2)
                    split_chunk(g, KCH[s])
                    split_chunk(g, GCH[s])

            load_decay(0, 0)
            load_decay(1, 1)
            for m in range(XCH + AHEAD):
                arrived(act, 0, m)
                nc.scalar.activation(split_dst(m, xh, wh), raw[:, m % RAW, :], ACT.Copy)\
                    .then_inc(split_hi, 1)
            act.wait_ge(const_in, CONSTS * 16)
            nc.scalar.activation(rh[:, :, :], rw[:, :, :], ACT.Copy).then_inc(router_hi, 1)
            group(0, True)
            with act.Fori(1, GROUPS) as g:
                group(g, False)
            attention(GROUPS, 0)

            def transposed(t):
                act.wait_ge(tr_done, t + 1)
                nc.scalar.activation(xh[:, :, tile(t)], ps[:, AO_B + t % 2, :].rearrange("p (k n) -> p k n", k=KT),
                                     ACT.Copy).then_inc(tr_hi, 1)

            def exponent(f):
                act.wait_ge(shifted, f + 1)
                nc.scalar.activation(prob[:, :, :], prob[:, :, :], ACT.Exp).then_inc(exp_done, 1)

            def lora_transposed(f):
                act.wait_ge(ht_done, f + 1)
                nc.scalar.activation(qh[:, half(f)], ps[:, AO_B, :], ACT.Copy).then_inc(ht_hi, 1)

            for t in range(4):
                transposed(t)
            exponent(0)
            for t in range(4, TT):
                transposed(t)
            lora_transposed(0)
            exponent(1)
            lora_transposed(1)
            for i in range(2):
                act.wait_ge(dec_in[i], 16 * (HEADS // 2 + 1))

        @block.vector
        def _(dve):
            def minus(dst, full, hi):
                return nc.vector.tensor_tensor(dst, full, f32(hi), ALU.subtract)

            def split_chunk(g, u):
                dve.wait_ge(split_hi, g * NCH + (XCH + AHEAD + u + 1))
                minus(wl[:, u % AHEAD, :], raw[:, (XCH + AHEAD + u) % RAW, :], wh[:, u % AHEAD, :])\
                    .then_inc(split_lo, 1)

            def front(g, i):
                n = silu_no(i)
                dve.wait_ge(sig_done, g * NSILU + (n + 1))
                nc.vector.tensor_tensor(sig[:, n % 2, :], ps[:, PROJ_B + i % 4, :], sig[:, n % 2, :], ALU.mult)\
                    .then_inc(silu_full, 1)

            def back(g, i, hi, lo):
                n = silu_no(i)
                dve.wait_ge(silu_hi, g * NSILU + (n + 1))
                minus(lo, sig[:, n % 2, :], hi).then_inc(silu_lo, 1)

            def mask(g, s, b):
                n = s * BATCH + b
                if n >= 2 or not isinstance(g, int):
                    dve.wait_ge(s_lo, g * (HG * BATCH) + (n - 1))
                dve.wait_ge(s_done, g * (HG * BATCH) + (n + 1))
                nc.vector.tensor_tensor(sfull[:, b % 2, :], ps[:, S_B + b % 2, 0:SC], dec[:, s % 2, :], ALU.mult)\
                    .then_inc(s_full, 1)

            def scores_lo(g, s, b):
                dve.wait_ge(s_hi, g * (HG * BATCH) + (s * BATCH + b + 1))
                minus(sl[:, b, :], sfull[:, b % 2, :], sh[:, b, :]).then_inc(s_lo, 1)

            def scores(g, s):
                dve.wait_ge(dec_in[s % 2], g * (16 * HG // 2) + 16 * (s // 2 + 1))
                mask(g, s, 0)
                mask(g, s, 1)
                for b in range(BATCH):
                    scores_lo(g, s, b)
                    if b + 2 < BATCH:
                        mask(g, s, b + 2)

            def attention(g, s):
                r = (s - 1) % HG
                for e in range(2):
                    a = 2 * (s - 1) + e
                    dve.wait_ge(sq_done, g * (2 * HG) + (a + 1))
                    dve.wait_ge(gate_done, g * NGATE + (a + 1))
                    h = g * HG + (s - 1)
                    scale = nw[:, h:h + 1] if isinstance(h, int) else nw[:, bass.ds(h, 1)]
                    nc.vector.scalar_tensor_tensor(out=gate[:, e, :], in0=ps[:, AO_B + e, :], scalar=scale,
                                                   in1=gate[:, e, :], op0=ALU.mult, op1=ALU.mult)\
                        .then_inc(y_full, 1)
                for e in range(2):
                    a = 2 * (s - 1) + e
                    dve.wait_ge(sq_added, g * (2 * HG) + (a + 1))
                    nc.vector.tensor_tensor(sqacc[:, e, :], sqacc[:, e, :], sq[:, e, :], ALU.add)\
                        .then_inc(sq_added, 1)
                    dve.wait_ge(y_hi, g * (2 * HG) + (a + 1))
                    minus(yl[:, r, half(e)], gate[:, e, :], yh[:, r, half(e)]).then_inc(y_lo, 1)

            def output(g, t):
                dve.wait_ge(o_done, g * TT + (t - TT + 1))
                dve.wait_ge(o_added, g * TT + (t + 1 - TT))
                nc.vector.tensor_tensor(acc[:, t, :], acc[:, t, :], ps[:, AO_B + t % 2, :], ALU.add)\
                    .then_inc(o_added, 1)

            def group(g, first):
                for s in range(HG):
                    q, k = QJOB[s], KJOB[s]
                    front(g, q)
                    front(g, q + 1)
                    back(g, q, qh[:, half(0)], ql[:, half(0)])
                    split_chunk(g, QCH[s])
                    back(g, q + 1, qh[:, half(1)], ql[:, half(1)])
                    if s == 1 and not first:
                        for t in range(TT):
                            output(g, t)
                    if s > 0 or not first:
                        attention(g, s)
                    if s == 0:
                        for t in range(TT):
                            front(g, VJOB + t)
                            if t:
                                back(g, VJOB + t - 1, vh[:, t - 1, :], vl[:, t - 1, :])
                        front(g, k)
                        back(g, VJOB + TT - 1, vh[:, TT - 1, :], vl[:, TT - 1, :])
                    else:
                        front(g, k)
                    c = {0: VCH, 1: OCH}.get(s)
                    if c is not None:
                        split_chunk(g, c)
                    front(g, k + 1)
                    back(g, k, kh[:, half(0)], kl[:, half(0)])
                    back(g, k + 1, kh[:, half(1)], kl[:, half(1)])
                    if c is not None:
                        split_chunk(g, c + 1)
                        split_chunk(g, c + 2)
                        split_chunk(g, c + 3)
                    scores(g, s)
                    split_chunk(g, KCH[s])
                    split_chunk(g, GCH[s])

            nc.vector.memset(sqacc[:, :, :], 0.0).then_inc(sq_added, 2)
            nc.vector.memset(acc[:, :, :], 0.0).then_inc(o_added, TT)
            for m in range(XCH + AHEAD):
                dve.wait_ge(split_hi, m + 1)
                minus(split_dst(m, xl, wl), raw[:, m % RAW, :], split_dst(m, xh, wh)).then_inc(split_lo, 1)
            dve.wait_ge(router_hi, 1)
            minus(rl[:, :, :], rw[:, :, :], rh[:, :, :]).then_inc(router_lo, 1)
            dve.wait_ge(const_in, CONSTS * 16)
            group(0, True)
            with dve.Fori(1, GROUPS) as g:
                group(g, False)
            attention(GROUPS, 0)

            steps = [0]

            def link(ins):
                steps[0] += 1
                ins.then_inc(dve_step, 1)
                dve.wait_ge(dve_step, steps[0])

            def rsqrt(dst, v):
                link(nc.vector.tensor_scalar(dst.bitcast(I32), v.bitcast(I32), -0.5, float(0x5f3759df),
                                             ALU.mult, ALU.add))
                t = rs_t[:, 0:v.shape[1]]
                for _ in range(4):
                    link(nc.vector.tensor_tensor(t, dst, dst, ALU.mult))
                    link(nc.vector.scalar_tensor_tensor(out=t, in0=t, scalar=-0.5, in1=v, op0=ALU.mult, op1=ALU.mult))
                    link(nc.vector.scalar_tensor_tensor(out=dst, in0=t, scalar=1.5, in1=dst, op0=ALU.add,
                                                        op1=ALU.mult))

            def moments(t):
                link(nc.vector.bn_stats(stat[:, t, :], acc[:, t, :]))
                link(nc.vector.bn_aggr(mv[:, t, :], stat[:, t, :]))

            def inverse_deviation(t0, n):
                link(nc.vector.tensor_scalar(rs_v[:, t0:t0 + n], mv[:, t0:t0 + n, 1], EPS, None, ALU.add))
                rsqrt(rstd[:, t0:t0 + n], rs_v[:, t0:t0 + n])

            def normalize(t):
                return nc.vector.tensor_scalar(acc[:, t, :], acc[:, t, :], mv[:, t, 0:1], rstd[:, t:t + 1],
                                               ALU.subtract, ALU.mult)

            def first_residual(t):
                m = NSTREAM + t
                output(GROUPS, t)
                dve.wait_ge(o_added, GROUPS * TT + t + 1)
                arrived(dve, 0, m)
                ins = nc.vector.scalar_tensor_tensor(out=acc[:, t, :], in0=acc[:, t, :], scalar=rms[:, t:t + 1],
                                                     in1=raw[:, m % RAW, :], op0=ALU.mult, op1=ALU.add)
                ins.then_inc(x1_done, 1)
                dve.wait_ge(x1_done, t + 1)
                moments(t)

            def transposed(t):
                dve.wait_ge(tr_hi, t + 1)
                minus(xl[:, :, tile(t)], ps[:, AO_B + t % 2, :].rearrange("p (k n) -> p k n", k=KT),
                      xh[:, :, tile(t)]).then_inc(tr_lo, 1)

            def router(f):
                dve.wait_ge(hl_done, f + 1)
                lg = ps[:, S_B, :].rearrange("p (t n) -> p t n", t=4)[:, :, 0:NROUTE]
                link(nc.vector.tensor_tensor(prob[:, :, :], lg, rb[:, :].unsqueeze(1).broadcast_to([P, 4, NROUTE]), ALU.add))
                link(nc.vector.tensor_reduce(red[:, :], prob[:, :, :], AX.X, ALU.max))
                nc.vector.tensor_tensor(prob[:, :, :], prob[:, :, :], red[:, :].unsqueeze(2).broadcast_to([P, 4, NROUTE]),
                                        ALU.subtract).then_inc(shifted, 1)
                dve.wait_ge(exp_done, f + 1)
                link(nc.vector.tensor_reduce(red[:, :], prob[:, :, :], AX.X, ALU.add))
                link(nc.vector.reciprocal(red[:, :], red[:, :]))
                link(nc.vector.tensor_tensor(prob[:, :, :], prob[:, :, :], red[:, :].unsqueeze(2).broadcast_to([P, 4, NROUTE]),
                                             ALU.mult))
                pj = prob[:, :, :].unsqueeze(2).broadcast_to([P, 4, NROUTE, NROUTE])
                pi = prob[:, :, :].unsqueeze(3).broadcast_to([P, 4, NROUTE, NROUTE])
                later = order[:, 0:1, :, :].broadcast_to([P, 4, NROUTE, NROUTE])
                earlier = order[:, 1:2, :, :].broadcast_to([P, 4, NROUTE, NROUTE])
                link(nc.vector.tensor_tensor(cmp_a[:, :, :, :], pj, pi, ALU.is_gt))
                link(nc.vector.tensor_tensor(cmp_b[:, :, :, :], pj, pi, ALU.is_ge))
                link(nc.vector.tensor_tensor(cmp_a[:, :, :, :], cmp_a[:, :, :, :], later, ALU.mult))
                link(nc.vector.tensor_tensor(cmp_b[:, :, :, :], cmp_b[:, :, :, :], earlier, ALU.mult))
                link(nc.vector.tensor_tensor(cmp_a[:, :, :, :], cmp_a[:, :, :, :], cmp_b[:, :, :, :], ALU.add))
                link(nc.vector.tensor_reduce(rank[:, :, :], cmp_a[:, :, :, :], AX.X, ALU.add))
                link(nc.vector.scalar_tensor_tensor(out=prob[:, :, :], in0=rank[:, :, :], scalar=float(NEXP),
                                                    in1=prob[:, :, :], op0=ALU.is_lt, op1=ALU.mult))
                link(nc.vector.tensor_tensor(wexp[:, :, :, :], prob[:, :, :].unsqueeze(2).broadcast_to([P, 4, NEXP, NROUTE]),
                                             route[:, :, :].unsqueeze(1).broadcast_to([P, 4, NEXP, NROUTE]), ALU.mult))
                link(nc.vector.tensor_reduce(wsum[:, :, :], wexp[:, :, :, :], AX.X, ALU.add))
                nc.vector.tensor_tensor(hw[:, :, :].rearrange("p t (e r) -> p t e r", e=NEXP),
                                        ps[:, S_B + 1, :].rearrange("p (t e r) -> p t e r", t=4, e=NEXP),
                                        wsum[:, :, :].unsqueeze(3).broadcast_to([P, 4, NEXP, RANK]), ALU.mult).then_inc(hw_done, 1)

            def lora_transposed(f):
                dve.wait_ge(ht_hi, f + 1)
                minus(ql[:, half(f)], ps[:, AO_B, :], qh[:, half(f)]).then_inc(ht_lo, 1)

            def second_residual(t):
                dve.wait_ge(ffn_done, t + 1)
                dve.wait_ge(bias_added, t + 1)
                nc.vector.tensor_tensor(acc[:, t, :], acc[:, t, :], ps[:, PROJ_B + t % 4, :], ALU.add)\
                    .then_inc(ffn_read, 1)
                dve.wait_ge(ffn_read, t + 1)
                moments(t)

            for e in range(NEXP):
                link(nc.vector.tensor_scalar(route[:, e, :], emap[:, :], float(e), SCALING, ALU.is_equal, ALU.mult))
            dve.wait_ge(ss_done, 1)
            link(nc.vector.tensor_scalar(rs_v[:, :], ps[:, S_B, 0:TT], 1.0 / (HEADS * P), EPS, ALU.mult, ALU.add))
            rsqrt(rms[:, :], rs_v[:, :])
            for t in range(4):
                first_residual(t)
            inverse_deviation(0, 4)
            for t in range(4):
                normalize(t).then_inc(ln1_done, 1)
            first_residual(4)
            first_residual(5)
            for t in range(4):
                transposed(t)
            first_residual(6)
            first_residual(7)
            inverse_deviation(4, 4)
            for t in range(4, TT):
                normalize(t).then_inc(ln1_done, 1)
            router(0)
            for t in range(4, TT):
                transposed(t)
            lora_transposed(0)
            router(1)
            for f in range(2):
                for t in range(4 * f, 4 * f + 4):
                    second_residual(t)
                inverse_deviation(4 * f, 4)
                for t in range(4 * f, 4 * f + 4):
                    normalize(t).then_inc(out_ready, 1)
                if f == 0:
                    lora_transposed(1)

        @block.gpsimd
        def _(pool):
            pool.wait_ge(const_in, CONSTS * 16)
            for t in range(TT):
                pool.wait_ge(tr_done, t + 1)
                nc.gpsimd.tensor_tensor(acc[:, t, :], acc[:, t, :], bb[:, :], ALU.add).then_inc(bias_added, 1)

        @block.tensor
        def _(pe):
            def mm3(dst, wt, mv_, start, stop):
                nc.tensor.matmul(dst, wt[0], mv_[0], start=start, stop=False)
                nc.tensor.matmul(dst, wt[0], mv_[1], start=False, stop=False)
                return nc.tensor.matmul(dst, wt[1], mv_[0], start=False, stop=stop)

            def chunk_ready(g, n):
                pe.wait_ge(split_lo, g * NCH + (XCH + n + 1))

            def bank_free(g, i):
                j, back = (i - 4, 0) if i >= 4 else (i - 4 + NPROJ, 1)
                if back and isinstance(g, int):
                    return
                if PROJ[j] == "g":
                    pe.wait_ge(gate_done, g * NGATE + (gate_no(j) + 1 - back * NGATE))
                else:
                    pe.wait_ge(silu_full, g * NSILU + (silu_no(j) + 1 - back * NSILU))

            def project(g, i, c, e):
                bank_free(g, i)
                r = c % AHEAD
                for k in range(KT):
                    last = mm3(ps[:, PROJ_B + i % 4, :], (wh[:, r, tile(k)], wl[:, r, tile(k)]),
                               (xh[:, k, half(e)], xl[:, k, half(e)]), k == 0, k == KT - 1)
                last.then_inc(proj_done, 1)

            def both_halves(g, i, c):
                chunk_ready(g, c)
                project(g, i, c, 0)
                project(g, i + 1, c, 1)

            def values(g):
                for k in range(KT):
                    chunk_ready(g, VCH + k)
                for t in range(TT):
                    i = VJOB + t
                    bank_free(g, i)
                    for k in range(KT):
                        r = (VCH + k) % AHEAD
                        last = mm3(ps[:, PROJ_B + i % 4, :], (xh[:, k, tile(t)], xl[:, k, tile(t)]),
                                   (wh[:, r, :], wl[:, r, :]), k == 0, k == KT - 1)
                    last.then_inc(proj_done, 1)

            def scores(g, s):
                pe.wait_ge(silu_lo, g * NSILU + (silu_no(KJOB[s] + 1) + 1))
                for b in range(BATCH):
                    n = s * BATCH + b
                    if n >= 2 or not isinstance(g, int):
                        pe.wait_ge(s_full, g * (HG * BATCH) + (n - 1))
                    q0 = b * SEQ
                    mm3(ps[:, S_B + b % 2, 0:SEQ], (kh[:, q0:q0 + P], kl[:, q0:q0 + P]),
                        (qh[:, q0:q0 + SEQ], ql[:, q0:q0 + SEQ]), True, True)
                    mm3(ps[:, S_B + b % 2, SEQ:SC], (kh[:, q0 + P:q0 + SEQ], kl[:, q0 + P:q0 + SEQ]),
                        (qh[:, q0 + P:q0 + SEQ], ql[:, q0 + P:q0 + SEQ]), True, True)\
                        .then_inc(s_done, 1)

            def attention(g, s):
                r = (s - 1) % HG
                hs = slice(r * P, r * P + P)
                for e in range(2):
                    a = 2 * (s - 1) + e
                    if a >= 2 or not isinstance(g, int) or g > 0:
                        pe.wait_ge(y_full, g * (2 * HG) + (a - 1))
                    if s == 1 and not isinstance(g, int):
                        pe.wait_ge(o_added, g * TT + (TT - 1 + e))
                    for b in (2 * e, 2 * e + 1):
                        pe.wait_ge(s_lo, g * (HG * BATCH) + ((s - 1) * BATCH + b + 1))
                        o = (b % 2) * SEQ
                        mm3(ps[:, AO_B + e, o:o + SEQ], (vh[:, 2 * b, hs], vl[:, 2 * b, hs]),
                            (sh[:, b, 0:SEQ], sl[:, b, 0:SEQ]), True, False)
                        last = mm3(ps[:, AO_B + e, o + P:o + SEQ], (vh[:, 2 * b + 1, hs], vl[:, 2 * b + 1, hs]),
                                   (sh[:, b, SEQ:SC], sl[:, b, SEQ:SC]), False, True)
                    last.then_inc(att_done, 1)

            def output(g, t, ch0):
                if t < 2:
                    pe.wait_ge(y_lo, g * (2 * HG))
                elif not (isinstance(g, int) and t >= 6):
                    pe.wait_ge(o_added, g * TT + (t - 1))
                for hh in range(HG):
                    r = (ch0 + hh) % AHEAD
                    last = mm3(ps[:, AO_B + t % 2, :], (yh[:, hh, tile(t)], yl[:, hh, tile(t)]),
                               (wh[:, r, :], wl[:, r, :]), hh == 0, hh == HG - 1)
                last.then_inc(o_done, 1)

            def group(g, first):
                for s in range(HG):
                    if s == 0 and first:
                        pe.wait_ge(split_lo, KT + 1)
                        project(g, 0, 0, 0)
                        pe.wait_ge(split_lo, XCH + 1)
                        project(g, 1, 0, 1)
                    else:
                        both_halves(g, QJOB[s], QCH[s])
                    if s == 1 and not first:
                        chunk_ready(g, OCH + HG - 1)
                        for t in range(TT):
                            output(g, t, OCH)
                    if s > 0 or not first:
                        attention(g, s)
                    if s == 0:
                        values(g)
                    both_halves(g, KJOB[s], KCH[s])
                    both_halves(g, GJOB[s], GCH[s])
                    scores(g, s)

            group(0, True)
            with pe.Fori(1, GROUPS) as g:
                group(g, False)

            def sum_of_squares():
                pe.wait_ge(sq_added, 2 + 2 * HEADS)
                for t in range(TT):
                    last = nc.tensor.matmul(ps[:, S_B, t:t + 1], sqacc[:, t // 4, tile(t % 4)], ones[:, 0:1],
                                            start=True, stop=True)
                last.then_inc(ss_done, 1)

            def transposed(t):
                pe.wait_ge(ln1_done, t + 1)
                if t in (0, 1):
                    pe.wait_ge(o_added, GROUPS * TT + 5 + t)
                elif t in (4, 5):
                    pe.wait_ge(o_added, GROUPS * TT + 3 + t)
                else:
                    pe.wait_ge(tr_lo, t - 1)
                for k in range(KT):
                    last = nc.tensor.transpose(ps[:, AO_B + t % 2, tile(k)], acc[:, t, tile(k)], ident[:, :])
                last.then_inc(tr_done, 1)

            def router_and_lora(f):
                if f:
                    pe.wait_ge(hw_done, f)
                for t in range(4 * f, 4 * f + 4):
                    pe.wait_ge(tr_lo, t + 1)
                    q = t % 4
                    for k in range(KT):
                        xt = (xh[:, k, tile(t)], xl[:, k, tile(t)])
                        mm3(ps[:, S_B, q * P:q * P + RANK], xt, (rh[:, k, :], rl[:, k, :]), k == 0, k == KT - 1)
                    for k in range(KT):
                        xt = (xh[:, k, tile(t)], xl[:, k, tile(t)])
                        last = mm3(ps[:, S_B + 1, tile(q)], xt, (wh[:, ACH, tile(k)], wl[:, ACH, tile(k)]),
                                   k == 0, k == KT - 1)
                last.then_inc(hl_done, 1)

            def base(t):
                if t >= 4:
                    pe.wait_ge(ffn_read, t - 3)
                for k in range(KT):
                    mm3(ps[:, PROJ_B + t % 4, :], (xh[:, k, tile(t)], xl[:, k, tile(t)]),
                        (wh[:, BASECH + k, :], wl[:, BASECH + k, :]), k == 0, False)

            def lora(t):
                mm3(ps[:, PROJ_B + t % 4, :], (qh[:, tile(t)], ql[:, tile(t)]), (wh[:, BCH, :], wl[:, BCH, :]),
                    False, True).then_inc(ffn_done, 1)

            def lora_transposed(f):
                pe.wait_ge(hw_done, f + 1)
                if f:
                    pe.wait_ge(ht_lo, f)
                else:
                    pe.wait_ge(tr_lo, TT - 1)
                for q in range(4):
                    last = nc.tensor.transpose(ps[:, AO_B, tile(q)], hw[:, q, :], ident[:, :])
                last.then_inc(ht_done, 1)

            attention(GROUPS, 0)
            chunk_ready(GROUPS, TAIL_OCH + HG - 1)
            output(GROUPS, 0, TAIL_OCH)
            output(GROUPS, 1, TAIL_OCH)
            sum_of_squares()
            for t in range(2, 6):
                output(GROUPS, t, TAIL_OCH)
            for t in range(4):
                transposed(t)
            for t in (6, 7):
                pe.wait_ge(tr_lo, t - 3)
                output(GROUPS, t, TAIL_OCH)
            pe.wait_ge(router_lo, 1)
            chunk_ready(GROUPS, BCH)
            router_and_lora(0)
            for t in range(4):
                base(t)
            for t in range(4, TT):
                transposed(t)
            router_and_lora(1)
            lora_transposed(0)
            pe.wait_ge(ht_lo, 1)
            for t in range(4):
                lora(t)
            for t in range(4, TT):
                base(t)
            lora_transposed(1)
            pe.wait_ge(ht_lo, 2)
            for t in range(4, TT):
                lora(t)


def decay_tables():
    f = np.float32
    base = f(1.0 / 2.0 ** (8.0 / HEADS))
    factor = f(1.0 - 1 / (32 - 1 + 1e-05) + 1e-05)
    slope = (base ** (np.arange(HEADS, dtype=f) + f(1)) * factor).astype(np.float64)
    d = np.arange(SEQ)[None, :] - np.arange(P)[:, None]
    table = np.where(d >= 0, np.exp(-slope[:, None, None] * np.maximum(d, 0)), 0.0).astype(f)
    table = np.concatenate([table, table[:, :, :P]], axis=2)
    return np.concatenate([table, table[:2]], axis=0)


def kernel(L0_attn_hidden_states, L0_attn_qkv_w, L0_attn_out_w, L0_attn_gate_w, L0_attn_norm_w, L0_ffn_base_W,
           L0_ffn_base_b, L0_ffn_router_W, L0_ffn_router_b, L0_ffn_A, L0_ffn_B, L0_ffn_expert_map):
    from concourse import bacc
    from concourse.bass_utils import run_bass_kernel_spmd

    x = np.ascontiguousarray(L0_attn_hidden_states).reshape(TOK, HID)
    qkv = np.asarray(L0_attn_qkv_w).reshape(HEADS, 3, P, KT, P)
    gate = np.asarray(L0_attn_gate_w).reshape(HEADS, P, KT, P)

    def per_head(w):
        return w.transpose(0, 3, 2, 1).reshape(HEADS, P, W)

    wq, wk, wg = per_head(qkv[:, 0]), per_head(qkv[:, 1]), per_head(gate)
    wv = qkv[:, 2].reshape(GROUPS, HG, P, KT, P).transpose(0, 3, 4, 1, 2).reshape(GROUPS, KT, P, W)
    wo = np.asarray(L0_attn_out_w).reshape(HID, HEADS, P).transpose(1, 2, 0)
    xt = x.reshape(2, W, KT, P).transpose(0, 2, 3, 1).reshape(XCH, P, W)
    chunks = []
    for g in range(GROUPS):
        place = {"q": 0, "k": 0, "g": 0, "v": 0, "o": 0}
        for kind in CHUNKS:
            n = place[kind]
            place[kind] += 1
            if kind == "v":
                chunks.append(wv[g, n])
            elif kind == "o":
                chunks.append(wo[HG * (g - 1) + n] if g else np.zeros_like(wo[0]))
            else:
                chunks.append({"q": wq, "k": wk, "g": wg}[kind][HG * g + n])
    chunks += list(wo[HEADS - HG:])
    chunks += list(np.asarray(L0_ffn_base_W).reshape(HID, KT, P).transpose(1, 2, 0))
    chunks.append(np.asarray(L0_ffn_A).reshape(NEXP * RANK, KT, P).transpose(2, 1, 0).reshape(P, W))
    chunks.append(np.asarray(L0_ffn_B).transpose(0, 2, 1).reshape(NEXP * RANK, HID))
    stream = np.stack(list(xt[:KT]) + chunks[:1] + list(xt[KT:]) + chunks[1:])
    router = np.zeros((P, KT, RANK), np.float32)
    router[:, :, :NROUTE] = np.asarray(L0_ffn_router_W).reshape(NROUTE, KT, P).transpose(2, 1, 0)
    i = np.arange(NROUTE)
    order = np.stack([i[None, :] > i[:, None], i[None, :] < i[:, None]]).astype(np.float32)
    arrays = {
        "stream": stream, "x": x, "decay": decay_tables(),
        "norm_w": np.asarray(L0_attn_norm_w).reshape(HEADS, P).T,
        "base_b": np.asarray(L0_ffn_base_b), "router_w": router, "router_b": np.asarray(L0_ffn_router_b),
        "expert_map": np.asarray(L0_ffn_expert_map),
        "ident_in": np.eye(P, dtype=np.float32), "ones_in": np.ones((P, 2), np.float32), "order_in": order,
    }
    arrays = {n: np.ascontiguousarray(a) for n, a in arrays.items()}
    nc = bacc.Bacc("TRN2", target_bir_lowering=False, num_devices=1, dynamic_dma_scratch_size=1024)
    args = {n: nc.dram_tensor(n, a.shape, mybir.dt.from_np(a.dtype), kind="ExternalInput").ap()
            for n, a in arrays.items()}
    out = nc.dram_tensor("out", (TOK, HID), FP32, kind="ExternalOutput").ap()
    build(nc, out=out, **args)
    r = run_bass_kernel_spmd(nc, [arrays], core_ids=[0])
    return r.results[0]["out"].reshape(L0_attn_hidden_states.shape)
```

```python
import numpy as np
import concourse.bass as bass
from concourse import mybir
from concourse.alu_op_type import AluOpType as ALU
from contextlib import ExitStack

FP32 = mybir.dt.float32
FP32R = mybir.dt.float32r
I32 = mybir.dt.int32
ACT = mybir.ActivationFunctionType
AX = mybir.AxisListType

P = 128
BATCH, SEQ, HID = 4, 256, 512
TOK = BATCH * SEQ
TT = TOK // P
HEADS, BLOCK = 32, 32
KT = HID // P
HG = 4
GROUPS = HEADS // HG
W = 512
SC = SEQ + P
NEXP, NROUTE, RANK = 8, 15, 16
SCALING = 2.0
EPS = 1e-5

CHUNKS = (["q", "k", "v", "v", "v", "v", "g"] + ["q", "k", "o", "o", "o", "o", "g"]
          + ["q", "k", "g"] + ["q", "k", "g"])
NCH = len(CHUNKS)
QCH = [0, 7, 14, 17]
KCH = [1, 8, 15, 18]
GCH = [6, 13, 16, 19]
VCH, OCH = 2, 9
AHEAD = 10
RAW = 5
XCH = 2 * KT
TAIL_OCH, BASECH, ACH, BCH = 0, 4, 8, 9
CONSTS = 8
NSTREAM = XCH + GROUPS * NCH + AHEAD

PROJ = ["q"] * 2 + ["k"] * 2 + ["v"] * TT + ["g"] * 2 + (["q"] * 2 + ["k"] * 2 + ["g"] * 2) * 3
NPROJ = len(PROJ)
NSILU = sum(j != "g" for j in PROJ)
NGATE = NPROJ - NSILU
QJOB, KJOB, GJOB, VJOB = [0, 14, 20, 26], [2, 16, 22, 28], [12, 18, 24, 30], 4
TAIL_BANK = [4, 5, 0, 1, 2, 3, 6, 7]


def silu_no(i):
    return sum(j != "g" for j in PROJ[:i])


def gate_no(i):
    return sum(j == "g" for j in PROJ[:i])


def build(nc, stream, x, decay, norm_w, base_b, router_w, router_b, expert_map, ident_in, ones_in, fresh_in, out):
    ctx = ExitStack()
    with ctx:
        def sb(name, shape, dt=FP32):
            return ctx.enter_context(nc.sbuf_tensor(name, shape, dt))

        def sem(name):
            return ctx.enter_context(nc.semaphore(name))

        raw = sb("raw", [P, RAW, W])
        wh = sb("wh", [P, AHEAD, W], FP32R)
        wl = sb("wl", [P, AHEAD, W], FP32R)
        xh = sb("xh", [P, KT, TOK], FP32R)
        xl = sb("xl", [P, KT, TOK], FP32R)
        qh = sb("qh", [P, TOK], FP32R)
        ql = sb("ql", [P, TOK], FP32R)
        kh = sb("kh", [P, TOK], FP32R)
        kl = sb("kl", [P, TOK], FP32R)
        vh = sb("vh", [P, TT, W], FP32R)
        vl = sb("vl", [P, TT, W], FP32R)
        sh = sb("sh", [P, BATCH, SC], FP32R)
        sl = sb("sl", [P, BATCH, SC], FP32R)
        yh = sb("yh", [P, HG, TOK], FP32R)
        yl = sb("yl", [P, HG, TOK], FP32R)
        sig = sb("sig", [P, 2, W])
        gate = sb("gate", [P, 2, W])
        sfull = sb("sfull", [P, 2, SC])
        sq = sb("sq", [P, 2, W])
        sqacc = sb("sqacc", [P, 2, W])
        acc = sb("acc", [P, TT, HID])
        dec = sb("dec", [P, 2, SC])
        nw = sb("nw", [P, HEADS])
        ident = sb("ident", [P, P])
        ones = sb("ones", [P, 2])
        rw = sb("rw", [P, KT, RANK])
        rh = sb("rh", [P, KT, RANK], FP32R)
        rl = sb("rl", [P, KT, RANK], FP32R)
        bb = sb("bb", [P, HID])
        rb = sb("rb", [P, NROUTE])
        emap = sb("emap", [P, NROUTE], I32)
        fresh = sb("fresh", [P, HG * NROUTE])
        route = sb("route", [P, NEXP, NROUTE])
        rms = sb("rms", [P, TT])
        meansq = sb("meansq", [P, TT])
        half_power = sb("half_power", [P, TT])
        stat = sb("stat", [P, 2 * TT, 6])
        mv = sb("mv", [P, 2 * TT, 2])
        var_eps = sb("var_eps", [P, 2 * TT])
        neg_mean = sb("neg_mean", [P, 2 * TT])
        rstd = sb("rstd", [P, 2 * TT])
        shift = sb("shift", [P, 2 * TT])
        prob = sb("prob", [P, HG, NROUTE])
        red = sb("red", [P, HG])
        top = sb("top", [P, HG, NEXP])
        above = sb("above", [P, HG, NROUTE])
        equal = sb("equal", [P, HG, NROUTE])
        taken = sb("taken", [P, HG, NROUTE])
        wexp = sb("wexp", [P, HG, NEXP, NROUTE])
        wsum = sb("wsum", [P, HG, NEXP])
        hw = sb("hw", [P, HG, P])
        ps = ctx.enter_context(nc.psum_tensor("ps", [P, 8, W], FP32))
        PROJ_B, S_B, AO_B = 0, 4, 6

        raw_in = [sem(f"raw_in{i}") for i in range(RAW)]
        dec_in = [sem(f"dec_in{i}") for i in range(2)]
        const_in = sem("const_in")
        stored = [sem(f"stored{t}") for t in range(TT)]
        split_hi, split_lo = sem("split_hi"), sem("split_lo")
        router_hi, router_lo = sem("router_hi"), sem("router_lo")
        proj_done, sig_done, silu_full = sem("proj_done"), sem("sig_done"), sem("silu_full")
        silu_hi, silu_lo, gate_done = sem("silu_hi"), sem("silu_lo"), sem("gate_done")
        s_done, s_full, s_hi, s_lo = sem("s_done"), sem("s_full"), sem("s_hi"), sem("s_lo")
        att_done, sq_done, sq_added = sem("att_done"), sem("sq_done"), sem("sq_added")
        y_full, y_hi, y_lo = sem("y_full"), sem("y_hi"), sem("y_lo")
        o_done, o_added = sem("o_done"), sem("o_added")
        ss_done, meansq_done, rms_done, power_set = sem("ss_done"), sem("meansq_done"), sem("rms_done"), sem("power_set")
        acc_scaled, x_added, x1_done, stats_done = sem("acc_scaled"), sem("x_added"), sem("x1_done"), sem("stats_done")
        affine_done, ln1_done, bias_added = sem("affine_done"), sem("ln1_done"), sem("bias_added")
        pool_step = sem("pool_step")
        tr_done, tr_hi, tr_lo = sem("tr_done"), sem("tr_hi"), sem("tr_lo")
        hl_done, shifted, exp_done, hw_done = sem("hl_done"), sem("shifted"), sem("exp_done"), sem("hw_done")
        ht_done, ht_hi, ht_lo = sem("ht_done"), sem("ht_hi"), sem("ht_lo")
        ffn_done, ffn_read, out_ready = sem("ffn_done"), sem("ffn_read"), sem("out_ready")
        dve_step = sem("dve_step")

        block = ctx.enter_context(nc.Block())

        def half(i):
            return slice(i * W, i * W + W)

        def tile(t):
            return slice(t * P, t * P + P)

        def f32(ap):
            return ap.bitcast(FP32)

        @block.sync
        def _(sp):
            def load(m):
                sp.dma_start(raw[:, m % RAW, :], stream[m]).then_inc(raw_in[m % RAW], 16)

            for m in range(XCH + 1):
                if m >= RAW:
                    sp.wait_ge(split_lo, m - RAW + 1)
                load(m)
            for dst, src in ((nw[:, :], norm_w), (ident[:, :], ident_in), (ones[:, :], ones_in),
                             (bb[:, :], base_b.partition_broadcast(P)), (rb[:, :], router_b.partition_broadcast(P)),
                             (emap[:, :], expert_map.partition_broadcast(P)), (rw[:, :, :], router_w),
                             (fresh[:, :], fresh_in.partition_broadcast(P))):
                sp.dma_start(dst, src).then_inc(const_in, 16)
            for m in range(XCH + 1, XCH + AHEAD):
                sp.wait_ge(split_lo, m - RAW + 1)
                load(m)
            with sp.Fori(0, GROUPS) as g:
                for j in range(NCH):
                    m0 = XCH + AHEAD + j
                    sp.wait_ge(split_lo, g * NCH + (m0 - RAW + 1))
                    src = stream[bass.ds(g * NCH + m0, 1), :, :].rearrange("a p n -> p (a n)")
                    sp.dma_start(raw[:, m0 % RAW, :], src).then_inc(raw_in[m0 % RAW], 16)
            for t in range(TT):
                m = NSTREAM + t
                if t < RAW:
                    sp.wait_ge(split_lo, m - RAW + 1)
                else:
                    sp.wait_ge(x_added, t - RAW + 1)
                sp.dma_start(raw[:, m % RAW, :], x[tile(t), :]).then_inc(raw_in[m % RAW], 16)
            for t in range(TT):
                sp.wait_ge(out_ready, t + 1)
                sp.dma_start(out[tile(t), :], acc[:, t, :]).then_inc(stored[t], 16)
            for t in range(TT):
                sp.wait_ge(stored[t], 16)

        def arrived(eng, g, m0):
            eng.wait_ge(raw_in[m0 % RAW], g * (16 * NCH // RAW) + 16 * (m0 // RAW + 1))

        def split_dst(m, xs, ws):
            if m == 0:
                return ws[:, 0, :]
            if m > XCH:
                return ws[:, m - XCH, :]
            return xs[:, (m - 1) % KT, half((m - 1) // KT)]

        @block.scalar
        def _(act):
            def load_decay(h, slot):
                src = decay[bass.ds(h, 1), :, :].rearrange("a p n -> p (a n)")
                act.dma_start(dec[:, slot, :], src).then_inc(dec_in[slot], 16)

            def split_chunk(g, u):
                arrived(act, g, XCH + AHEAD + u)
                s = CHUNKS[:u].count("g")
                if CHUNKS[u] != "o":
                    jobs = {"q": QJOB[s] + 2, "k": KJOB[s] + 2, "v": VJOB + TT, "g": GJOB[s] + 2}[CHUNKS[u]]
                    act.wait_ge(proj_done, g * NPROJ + jobs)
                elif not isinstance(g, int):
                    act.wait_ge(o_done, g * TT)
                nc.scalar.activation(wh[:, u % AHEAD, :], raw[:, (XCH + AHEAD + u) % RAW, :], ACT.Copy)\
                    .then_inc(split_hi, 1)

            def front(g, i):
                n = silu_no(i)
                act.wait_ge(proj_done, g * NPROJ + (i + 1))
                if n >= 2 or not isinstance(g, int):
                    act.wait_ge(silu_lo, g * NSILU + (n - 1))
                nc.scalar.activation(sig[:, n % 2, :], ps[:, PROJ_B + i % 4, :], ACT.Sigmoid).then_inc(sig_done, 1)

            def back(g, i, dst):
                n = silu_no(i)
                act.wait_ge(silu_full, g * NSILU + (n + 1))
                nc.scalar.activation(dst, sig[:, n % 2, :], ACT.Copy).then_inc(silu_hi, 1)

            def gate_half(g, s, e):
                i = GJOB[s] + e
                act.wait_ge(proj_done, g * NPROJ + (i + 1))
                if s > 0 or not isinstance(g, int):
                    act.wait_ge(y_lo, g * (2 * HG) + (2 * (s - 1) + e + 1))
                nc.scalar.activation(gate[:, e, :], ps[:, PROJ_B + i % 4, :], ACT.Sigmoid).then_inc(gate_done, 1)

            def scores(g, s, batches):
                for b in batches:
                    act.wait_ge(s_full, g * (HG * BATCH) + (s * BATCH + b + 1))
                    nc.scalar.activation(sh[:, b, :], sfull[:, b % 2, :], ACT.Copy).then_inc(s_hi, 1)

            def attention(g, s):
                r = (s - 1) % HG
                for e in range(2):
                    a = 2 * (s - 1) + e
                    act.wait_ge(att_done, g * (2 * HG) + (a + 1))
                    if a >= 2 or not isinstance(g, int) or g > 0:
                        act.wait_ge(sq_added, g * (2 * HG) + (a + 1))
                    nc.scalar.activation(sq[:, e, :], ps[:, AO_B + e, :], ACT.Square).then_inc(sq_done, 1)
                for e in range(2):
                    act.wait_ge(y_full, g * (2 * HG) + (2 * (s - 1) + e + 1))
                    nc.scalar.activation(yh[:, r, half(e)], gate[:, e, :], ACT.Copy).then_inc(y_hi, 1)

            def group(g, first):
                for s in range(HG):
                    q, k = QJOB[s], KJOB[s]
                    front(g, q)
                    front(g, q + 1)
                    back(g, q, qh[:, half(0)])
                    front(g, k)
                    back(g, q + 1, qh[:, half(1)])
                    front(g, k + 1)
                    back(g, k, kh[:, half(0)])
                    back(g, k + 1, kh[:, half(1)])
                    split_chunk(g, QCH[s])
                    split_chunk(g, KCH[s])
                    if s > 0 or not first:
                        attention(g, s)
                    if s == 0:
                        for t in range(TT):
                            front(g, VJOB + t)
                            if t:
                                back(g, VJOB + t - 1, vh[:, t - 1, :])
                        back(g, VJOB + TT - 1, vh[:, TT - 1, :])
                    gate_half(g, s, 0)
                    scores(g, s, (0, 1))
                    gate_half(g, s, 1)
                    scores(g, s, (2, 3))
                    load_decay(g * HG + (s + 2), s % 2)
                    for u in {0: range(VCH, VCH + KT), 1: range(OCH, OCH + HG)}.get(s, ()):
                        split_chunk(g, u)
                    split_chunk(g, GCH[s])

            load_decay(0, 0)
            load_decay(1, 1)
            for m in range(XCH + AHEAD):
                arrived(act, 0, m)
                nc.scalar.activation(split_dst(m, xh, wh), raw[:, m % RAW, :], ACT.Copy)\
                    .then_inc(split_hi, 1)
            act.wait_ge(const_in, CONSTS * 16)
            nc.scalar.activation(rh[:, :, :], rw[:, :, :], ACT.Copy).then_inc(router_hi, 1)
            group(0, True)
            with act.Fori(1, GROUPS) as g:
                group(g, False)
            attention(GROUPS, 0)

            def scale_acc(t):
                nc.scalar.activation(acc[:, t, :], acc[:, t, :], ACT.Copy, scale=rms[:, t:t + 1]).then_inc(acc_scaled, 1)

            def normalize(n, done):
                act.wait_ge(affine_done, n + 1)
                nc.scalar.activation(acc[:, n % TT, :], acc[:, n % TT, :], ACT.Identity, scale=rstd[:, n:n + 1],
                                     bias=shift[:, n:n + 1]).then_inc(done, 1)

            def transposed(t):
                act.wait_ge(tr_done, t + 1)
                nc.scalar.activation(xh[:, :, tile(t)], ps[:, 4 + t % 2, :].rearrange("p (k n) -> p k n", k=KT),
                                     ACT.Copy).then_inc(tr_hi, 1)

            def exponent(f):
                act.wait_ge(shifted, f + 1)
                nc.scalar.activation(prob[:, :, :], prob[:, :, :], ACT.Exp).then_inc(exp_done, 1)

            def lora_transposed(f):
                act.wait_ge(ht_done, f + 1)
                nc.scalar.activation(qh[:, half(f)], ps[:, 4, :], ACT.Copy).then_inc(ht_hi, 1)

            act.wait_ge(rms_done, 1)
            act.wait_ge(o_added, GROUPS * TT)
            for t in range(TT):
                scale_acc(t)
            for t in range(4):
                normalize(t, ln1_done)
            transposed(0)
            transposed(1)
            normalize(4, ln1_done)
            normalize(5, ln1_done)
            transposed(2)
            transposed(3)
            normalize(6, ln1_done)
            normalize(7, ln1_done)
            transposed(4)
            transposed(5)
            exponent(0)
            transposed(6)
            transposed(7)
            lora_transposed(0)
            exponent(1)
            for t in range(4):
                normalize(TT + t, out_ready)
            lora_transposed(1)
            for t in range(4, TT):
                normalize(TT + t, out_ready)
            for i in range(2):
                act.wait_ge(dec_in[i], 16 * (HEADS // 2 + 1))

        @block.vector
        def _(dve):
            def minus(dst, full, hi):
                return nc.vector.tensor_tensor(dst, full, f32(hi), ALU.subtract)

            def split_chunk(g, u):
                dve.wait_ge(split_hi, g * NCH + (XCH + AHEAD + u + 1))
                minus(wl[:, u % AHEAD, :], raw[:, (XCH + AHEAD + u) % RAW, :], wh[:, u % AHEAD, :])\
                    .then_inc(split_lo, 1)

            def front(g, i):
                n = silu_no(i)
                dve.wait_ge(sig_done, g * NSILU + (n + 1))
                nc.vector.tensor_tensor(sig[:, n % 2, :], ps[:, PROJ_B + i % 4, :], sig[:, n % 2, :], ALU.mult)\
                    .then_inc(silu_full, 1)

            def back(g, i, hi, lo):
                n = silu_no(i)
                dve.wait_ge(silu_hi, g * NSILU + (n + 1))
                minus(lo, sig[:, n % 2, :], hi).then_inc(silu_lo, 1)

            def mask(g, s, b):
                n = s * BATCH + b
                if n >= 2 or not isinstance(g, int):
                    dve.wait_ge(s_lo, g * (HG * BATCH) + (n - 1))
                dve.wait_ge(s_done, g * (HG * BATCH) + (n + 1))
                nc.vector.tensor_tensor(sfull[:, b % 2, :], ps[:, S_B + b % 2, 0:SC], dec[:, s % 2, :], ALU.mult)\
                    .then_inc(s_full, 1)

            def scores_lo(g, s, b):
                dve.wait_ge(s_hi, g * (HG * BATCH) + (s * BATCH + b + 1))
                minus(sl[:, b, :], sfull[:, b % 2, :], sh[:, b, :]).then_inc(s_lo, 1)

            def scores(g, s):
                dve.wait_ge(dec_in[s % 2], g * (16 * HG // 2) + 16 * (s // 2 + 1))
                for b in (0, 2):
                    mask(g, s, b)
                    mask(g, s, b + 1)
                    scores_lo(g, s, b)
                    scores_lo(g, s, b + 1)

            def attention(g, s):
                r = (s - 1) % HG
                for e in range(2):
                    a = 2 * (s - 1) + e
                    dve.wait_ge(sq_done, g * (2 * HG) + (a + 1))
                    dve.wait_ge(gate_done, g * NGATE + (a + 1))
                    h = g * HG + (s - 1)
                    scale = nw[:, h:h + 1] if isinstance(h, int) else nw[:, bass.ds(h, 1)]
                    nc.vector.scalar_tensor_tensor(out=gate[:, e, :], in0=ps[:, AO_B + e, :], scalar=scale,
                                                   in1=gate[:, e, :], op0=ALU.mult, op1=ALU.mult)\
                        .then_inc(y_full, 1)
                for e in range(2):
                    a = 2 * (s - 1) + e
                    dve.wait_ge(sq_added, g * (2 * HG) + (a + 1))
                    nc.vector.tensor_tensor(sqacc[:, e, :], sqacc[:, e, :], sq[:, e, :], ALU.add)\
                        .then_inc(sq_added, 1)
                    dve.wait_ge(y_hi, g * (2 * HG) + (a + 1))
                    minus(yl[:, r, half(e)], gate[:, e, :], yh[:, r, half(e)]).then_inc(y_lo, 1)

            def output(g, t):
                dve.wait_ge(o_done, g * TT + (t - TT + 1))
                dve.wait_ge(o_added, g * TT + (t + 1 - TT))
                nc.vector.tensor_tensor(acc[:, t, :], acc[:, t, :], ps[:, AO_B + t % 2, :], ALU.add)\
                    .then_inc(o_added, 1)

            def group(g, first):
                for s in range(HG):
                    q, k = QJOB[s], KJOB[s]
                    front(g, q)
                    front(g, q + 1)
                    back(g, q, qh[:, half(0)], ql[:, half(0)])
                    front(g, k)
                    back(g, q + 1, qh[:, half(1)], ql[:, half(1)])
                    front(g, k + 1)
                    back(g, k, kh[:, half(0)], kl[:, half(0)])
                    back(g, k + 1, kh[:, half(1)], kl[:, half(1)])
                    split_chunk(g, QCH[s])
                    split_chunk(g, KCH[s])
                    if s == 1 and not first:
                        for t in range(TT):
                            output(g, t)
                    if s > 0 or not first:
                        attention(g, s)
                    if s == 0:
                        for t in range(TT):
                            front(g, VJOB + t)
                            if t:
                                back(g, VJOB + t - 1, vh[:, t - 1, :], vl[:, t - 1, :])
                        back(g, VJOB + TT - 1, vh[:, TT - 1, :], vl[:, TT - 1, :])
                    scores(g, s)
                    for u in {0: range(VCH, VCH + KT), 1: range(OCH, OCH + HG)}.get(s, ()):
                        split_chunk(g, u)
                    split_chunk(g, GCH[s])

            nc.vector.memset(sqacc[:, :, :], 0.0).then_inc(sq_added, 2)
            nc.vector.memset(acc[:, :, :], 0.0).then_inc(o_added, TT)
            for m in range(XCH + AHEAD):
                dve.wait_ge(split_hi, m + 1)
                minus(split_dst(m, xl, wl), raw[:, m % RAW, :], split_dst(m, xh, wh)).then_inc(split_lo, 1)
            dve.wait_ge(router_hi, 1)
            minus(rl[:, :, :], rw[:, :, :], rh[:, :, :]).then_inc(router_lo, 1)
            dve.wait_ge(const_in, CONSTS * 16)
            group(0, True)
            with dve.Fori(1, GROUPS) as g:
                group(g, False)
            attention(GROUPS, 0)

            steps = [0]

            def link(ins):
                steps[0] += 1
                ins.then_inc(dve_step, 1)
                dve.wait_ge(dve_step, steps[0])

            def moments(n):
                link(nc.vector.bn_stats(stat[:, n, :], acc[:, n % TT, :]))
                nc.vector.bn_aggr(mv[:, n, :], stat[:, n, :]).then_inc(stats_done, 1)

            def first_residual(t):
                dve.wait_ge(o_done, (GROUPS - 1) * TT + t + 1)
                dve.wait_ge(x_added, t + 1)
                nc.vector.scalar_tensor_tensor(out=acc[:, t, :], in0=ps[:, TAIL_BANK[t], :], scalar=rms[:, t:t + 1],
                                               in1=acc[:, t, :], op0=ALU.mult, op1=ALU.add).then_inc(x1_done, 1)
                dve.wait_ge(x1_done, t + 1)
                moments(t)

            def transposed(t):
                dve.wait_ge(tr_hi, t + 1)
                minus(xl[:, :, tile(t)], ps[:, 4 + t % 2, :].rearrange("p (k n) -> p k n", k=KT),
                      xh[:, :, tile(t)]).then_inc(tr_lo, 1)

            def router(f):
                dve.wait_ge(hl_done, f + 1)
                each = [P, HG, NROUTE]
                lg = ps[:, 6, :].rearrange("p (t n) -> p t n", t=HG)[:, :, 0:NROUTE]
                link(nc.vector.tensor_tensor(prob[:, :, :], lg, rb[:, :].unsqueeze(1).broadcast_to(each), ALU.add))
                link(nc.vector.tensor_reduce(red[:, :], prob[:, :, :], AX.X, ALU.max))
                nc.vector.tensor_tensor(prob[:, :, :], prob[:, :, :], red[:, :].unsqueeze(2).broadcast_to(each),
                                        ALU.subtract).then_inc(shifted, 1)
                dve.wait_ge(exp_done, f + 1)
                link(nc.vector.tensor_reduce(red[:, :], prob[:, :, :], AX.X, ALU.add))
                link(nc.vector.reciprocal(red[:, :], red[:, :]))
                link(nc.vector.tensor_tensor(prob[:, :, :], prob[:, :, :],
                                             red[:, :].unsqueeze(2).broadcast_to(each), ALU.mult))
                for q in range(HG):
                    link(nc.vector.max(top[:, q, :], prob[:, q, :]))
                eighth = top[:, :, NEXP - 1:NEXP].broadcast_to(each)
                link(nc.vector.tensor_tensor(above[:, :, :], prob[:, :, :], eighth, ALU.is_gt))
                link(nc.vector.tensor_tensor(equal[:, :, :], prob[:, :, :], eighth, ALU.is_equal))
                link(nc.vector.tensor_reduce(red[:, :], above[:, :, :], AX.X, ALU.add))
                link(nc.vector.tensor_tensor_scan(taken[:, :, :].rearrange("p t n -> p (t n)"), fresh[:, :],
                                                  equal[:, :, :].rearrange("p t n -> p (t n)"), 0.0,
                                                  ALU.mult, ALU.add))
                link(nc.vector.tensor_tensor(taken[:, :, :], taken[:, :, :],
                                             red[:, :].unsqueeze(2).broadcast_to(each), ALU.add))
                link(nc.vector.scalar_tensor_tensor(out=equal[:, :, :], in0=taken[:, :, :], scalar=float(NEXP),
                                                    in1=equal[:, :, :], op0=ALU.is_le, op1=ALU.mult))
                link(nc.vector.tensor_tensor(above[:, :, :], above[:, :, :], equal[:, :, :], ALU.add))
                link(nc.vector.tensor_tensor(prob[:, :, :], prob[:, :, :], above[:, :, :], ALU.mult))
                link(nc.vector.tensor_tensor(wexp[:, :, :, :],
                                             prob[:, :, :].unsqueeze(2).broadcast_to([P, HG, NEXP, NROUTE]),
                                             route[:, :, :].unsqueeze(1).broadcast_to([P, HG, NEXP, NROUTE]), ALU.mult))
                link(nc.vector.tensor_reduce(wsum[:, :, :], wexp[:, :, :, :], AX.X, ALU.add))
                nc.vector.tensor_tensor(hw[:, :, :].rearrange("p t (e r) -> p t e r", e=NEXP),
                                        ps[:, 7, :].rearrange("p (t e r) -> p t e r", t=HG, e=NEXP),
                                        wsum[:, :, :].unsqueeze(3).broadcast_to([P, HG, NEXP, RANK]),
                                        ALU.mult).then_inc(hw_done, 1)

            def lora_transposed(f):
                dve.wait_ge(ht_hi, f + 1)
                minus(ql[:, half(f)], ps[:, 4, :], qh[:, half(f)]).then_inc(ht_lo, 1)

            def second_residual(t):
                dve.wait_ge(ffn_done, t + 1)
                dve.wait_ge(bias_added, t + 1)
                nc.vector.tensor_tensor(acc[:, t, :], acc[:, t, :], ps[:, t % 4, :], ALU.add).then_inc(ffn_read, 1)
                dve.wait_ge(ffn_read, t + 1)
                moments(TT + t)

            for e in range(NEXP):
                link(nc.vector.tensor_scalar(route[:, e, :], emap[:, :], float(e), SCALING, ALU.is_equal, ALU.mult))
            dve.wait_ge(ss_done, 1)
            nc.vector.tensor_scalar(meansq[:, :], ps[:, 7, 0:TT], 1.0 / (HEADS * P), EPS, ALU.mult, ALU.add)\
                .then_inc(meansq_done, 1)
            for t in range(4):
                first_residual(t)
            transposed(0)
            transposed(1)
            first_residual(4)
            first_residual(5)
            transposed(2)
            transposed(3)
            first_residual(6)
            first_residual(7)
            transposed(4)
            transposed(5)
            router(0)
            transposed(6)
            transposed(7)
            lora_transposed(0)
            router(1)
            for t in range(4):
                second_residual(t)
            lora_transposed(1)
            for t in range(4, TT):
                second_residual(t)

        @block.gpsimd
        def _(pool):
            steps = [0]

            def link(ins):
                steps[0] += 1
                ins.then_inc(pool_step, 1)
                pool.wait_ge(pool_step, steps[0])

            def affine(n):
                pool.wait_ge(stats_done, n + 1)
                nc.gpsimd.tensor_scalar(neg_mean[:, n:n + 1], mv[:, n, 0:1], -1.0, None, ALU.mult)
                link(nc.gpsimd.tensor_scalar(var_eps[:, n:n + 1], mv[:, n, 1:2], EPS, None, ALU.add))
                link(nc.gpsimd.tensor_tensor(rstd[:, n:n + 1], var_eps[:, n:n + 1], half_power[:, 0:1], ALU.pow))
                nc.gpsimd.tensor_tensor(shift[:, n:n + 1], neg_mean[:, n:n + 1], rstd[:, n:n + 1], ALU.mult)\
                    .then_inc(affine_done, 1)

            def add_x(t):
                m = NSTREAM + t
                pool.wait_ge(acc_scaled, t + 1)
                arrived(pool, 0, m)
                nc.gpsimd.tensor_tensor(acc[:, t, :], acc[:, t, :], raw[:, m % RAW, :], ALU.add).then_inc(x_added, 1)

            def add_bias(t):
                pool.wait_ge(tr_done, t + 1)
                nc.gpsimd.tensor_tensor(acc[:, t, :], acc[:, t, :], bb[:, :], ALU.add).then_inc(bias_added, 1)

            link(nc.gpsimd.memset(half_power[:, :], -0.5))
            pool.wait_ge(const_in, CONSTS * 16)
            pool.wait_ge(meansq_done, 1)
            nc.gpsimd.tensor_tensor(rms[:, :], meansq[:, :], half_power[:, :], ALU.pow).then_inc(rms_done, 1)
            add_x(0)
            add_x(1)
            for t in range(TT):
                if t + 2 < TT:
                    add_x(t + 2)
                affine(t)
            for t in range(TT):
                add_bias(t)
            for t in range(TT):
                affine(TT + t)

        @block.tensor
        def _(pe):
            def mm3(dst, wt, mv_, start, stop):
                nc.tensor.matmul(dst, wt[0], mv_[0], start=start, stop=False)
                nc.tensor.matmul(dst, wt[0], mv_[1], start=False, stop=False)
                return nc.tensor.matmul(dst, wt[1], mv_[0], start=False, stop=stop)

            def chunk_ready(g, n):
                pe.wait_ge(split_lo, g * NCH + (XCH + n + 1))

            def bank_free(g, i):
                j, back = (i - 4, 0) if i >= 4 else (i - 4 + NPROJ, 1)
                if back and isinstance(g, int):
                    return
                if PROJ[j] == "g":
                    pe.wait_ge(gate_done, g * NGATE + (gate_no(j) + 1 - back * NGATE))
                else:
                    pe.wait_ge(silu_full, g * NSILU + (silu_no(j) + 1 - back * NSILU))

            def project(g, i, c, e, ready=None):
                bank_free(g, i)
                r = c % AHEAD
                for k in range(KT):
                    if ready is not None:
                        ready(k)
                    last = mm3(ps[:, PROJ_B + i % 4, :], (wh[:, r, tile(k)], wl[:, r, tile(k)]),
                               (xh[:, k, half(e)], xl[:, k, half(e)]), k == 0, k == KT - 1)
                last.then_inc(proj_done, 1)

            def both_halves(g, i, c):
                chunk_ready(g, c)
                project(g, i, c, 0)
                project(g, i + 1, c, 1)

            def values(g):
                for k in range(KT):
                    chunk_ready(g, VCH + k)
                for t in range(TT):
                    i = VJOB + t
                    bank_free(g, i)
                    for k in range(KT):
                        r = (VCH + k) % AHEAD
                        last = mm3(ps[:, PROJ_B + i % 4, :], (xh[:, k, tile(t)], xl[:, k, tile(t)]),
                                   (wh[:, r, :], wl[:, r, :]), k == 0, k == KT - 1)
                    last.then_inc(proj_done, 1)

            def scores(g, s, batches):
                pe.wait_ge(silu_lo, g * NSILU + (silu_no(KJOB[s] + 1) + 1))
                for b in batches:
                    n = s * BATCH + b
                    if n >= 2 or not isinstance(g, int):
                        pe.wait_ge(s_full, g * (HG * BATCH) + (n - 1))
                    q0 = b * SEQ
                    mm3(ps[:, S_B + b % 2, 0:SEQ], (kh[:, q0:q0 + P], kl[:, q0:q0 + P]),
                        (qh[:, q0:q0 + SEQ], ql[:, q0:q0 + SEQ]), True, True)
                    mm3(ps[:, S_B + b % 2, SEQ:SC], (kh[:, q0 + P:q0 + SEQ], kl[:, q0 + P:q0 + SEQ]),
                        (qh[:, q0 + P:q0 + SEQ], ql[:, q0 + P:q0 + SEQ]), True, True)\
                        .then_inc(s_done, 1)

            def attention(g, s):
                r = (s - 1) % HG
                hs = slice(r * P, r * P + P)
                if s == 1:
                    pe.wait_ge(silu_lo, g * NSILU + (silu_no(VJOB + TT - 1) + 1))
                for e in range(2):
                    a = 2 * (s - 1) + e
                    if a >= 2 or not isinstance(g, int) or g > 0:
                        pe.wait_ge(y_full, g * (2 * HG) + (a - 1))
                    if s == 1 and not isinstance(g, int):
                        pe.wait_ge(o_added, g * TT + (TT - 1 + e))
                    for b in (2 * e, 2 * e + 1):
                        pe.wait_ge(s_lo, g * (HG * BATCH) + ((s - 1) * BATCH + b + 1))
                        o = (b % 2) * SEQ
                        mm3(ps[:, AO_B + e, o:o + SEQ], (vh[:, 2 * b, hs], vl[:, 2 * b, hs]),
                            (sh[:, b, 0:SEQ], sl[:, b, 0:SEQ]), True, False)
                        last = mm3(ps[:, AO_B + e, o + P:o + SEQ], (vh[:, 2 * b + 1, hs], vl[:, 2 * b + 1, hs]),
                                   (sh[:, b, SEQ:SC], sl[:, b, SEQ:SC]), False, True)
                    last.then_inc(att_done, 1)

            def output(g, t):
                if t < 2:
                    pe.wait_ge(y_lo, g * (2 * HG))
                else:
                    pe.wait_ge(o_added, g * TT + (t - 1))
                for hh in range(HG):
                    r = (OCH + hh) % AHEAD
                    last = mm3(ps[:, AO_B + t % 2, :], (yh[:, hh, tile(t)], yl[:, hh, tile(t)]),
                               (wh[:, r, :], wl[:, r, :]), hh == 0, hh == HG - 1)
                last.then_inc(o_done, 1)

            def group(g, first):
                for s in range(HG):
                    if s == 0 and first:
                        project(g, 0, 0, 0, ready=lambda k: pe.wait_ge(split_lo, k + 2))
                        pe.wait_ge(split_lo, XCH + 1)
                        project(g, 1, 0, 1)
                    else:
                        both_halves(g, QJOB[s], QCH[s])
                    both_halves(g, KJOB[s], KCH[s])
                    if s == 1 and not first:
                        chunk_ready(g, OCH + HG - 1)
                        for t in range(TT):
                            output(g, t)
                    if s > 0 or not first:
                        attention(g, s)
                    if s == 0:
                        values(g)
                    chunk_ready(g, GCH[s])
                    project(g, GJOB[s], GCH[s], 0)
                    scores(g, s, (0, 1))
                    project(g, GJOB[s] + 1, GCH[s], 1)
                    scores(g, s, (2, 3))

            group(0, True)
            with pe.Fori(1, GROUPS) as g:
                group(g, False)

            def tail_output(t, heads):
                for hh in heads:
                    last = mm3(ps[:, TAIL_BANK[t], :], (yh[:, hh, tile(t)], yl[:, hh, tile(t)]),
                               (wh[:, TAIL_OCH + hh, :], wl[:, TAIL_OCH + hh, :]), hh == 0, hh == HG - 1)
                return last

            def sum_of_squares():
                pe.wait_ge(sq_added, 2 + 2 * HEADS)
                pe.wait_ge(y_full, 2 * HEADS)
                for t in range(TT):
                    last = nc.tensor.matmul(ps[:, 7, t:t + 1], sqacc[:, t // 4, tile(t % 4)], ones[:, 0:1],
                                            start=True, stop=True)
                last.then_inc(ss_done, 1)

            def transposed(t):
                pe.wait_ge(ln1_done, t + 1)
                if t >= 2:
                    pe.wait_ge(tr_lo, t - 1)
                for k in range(KT):
                    last = nc.tensor.transpose(ps[:, 4 + t % 2, tile(k)], acc[:, t, tile(k)], ident[:, :])
                last.then_inc(tr_done, 1)

            def router_and_lora(f):
                if f:
                    pe.wait_ge(hw_done, f)
                else:
                    pe.wait_ge(x1_done, TT)
                for t in range(4 * f, 4 * f + 4):
                    pe.wait_ge(tr_lo, t + 1)
                    q = t % 4
                    for k in range(KT):
                        mm3(ps[:, 6, q * P:q * P + RANK], (xh[:, k, tile(t)], xl[:, k, tile(t)]),
                            (rh[:, k, :], rl[:, k, :]), k == 0, k == KT - 1)
                    for k in range(KT):
                        last = mm3(ps[:, 7, tile(q)], (xh[:, k, tile(t)], xl[:, k, tile(t)]),
                                   (wh[:, ACH, tile(k)], wl[:, ACH, tile(k)]), k == 0, k == KT - 1)
                last.then_inc(hl_done, 1)

            def base(t):
                pe.wait_ge(tr_lo, t + 1)
                if t < 4:
                    pe.wait_ge(x1_done, t + 3)
                else:
                    pe.wait_ge(ffn_read, t - 3)
                for k in range(KT):
                    mm3(ps[:, t % 4, :], (xh[:, k, tile(t)], xl[:, k, tile(t)]),
                        (wh[:, BASECH + k, :], wl[:, BASECH + k, :]), k == 0, False)

            def lora(t):
                mm3(ps[:, t % 4, :], (qh[:, tile(t)], ql[:, tile(t)]), (wh[:, BCH, :], wl[:, BCH, :]),
                    False, True).then_inc(ffn_done, 1)

            def lora_transposed(f):
                pe.wait_ge(hw_done, f + 1)
                pe.wait_ge(tr_lo, TT - 1)
                if f:
                    pe.wait_ge(ht_lo, f)
                for q in range(4):
                    last = nc.tensor.transpose(ps[:, 4, tile(q)], hw[:, q, :], ident[:, :])
                last.then_inc(ht_done, 1)

            pe.wait_ge(y_lo, 2 * (HEADS - 1))
            chunk_ready(GROUPS, TAIL_OCH + HG - 1)
            pe.wait_ge(gate_done, GROUPS * NGATE)
            first_heads = range(HG - 1)
            tail_output(2, first_heads)
            tail_output(3, first_heads)
            attention(GROUPS, 0)
            tail_output(4, first_heads)
            tail_output(5, first_heads)
            sum_of_squares()
            tail_output(0, first_heads)
            tail_output(1, first_heads)
            pe.wait_ge(y_lo, 2 * HEADS)
            for t in range(6):
                tail_output(t, [HG - 1]).then_inc(o_done, 1)
            pe.wait_ge(meansq_done, 1)
            for t in (6, 7):
                tail_output(t, range(HG)).then_inc(o_done, 1)
            pe.wait_ge(router_lo, 1)
            chunk_ready(GROUPS, BCH)
            transposed(0)
            transposed(1)
            base(0)
            transposed(2)
            transposed(3)
            base(1)
            transposed(4)
            transposed(5)
            router_and_lora(0)
            base(2)
            transposed(6)
            transposed(7)
            base(3)
            lora_transposed(0)
            router_and_lora(1)
            pe.wait_ge(ht_lo, 1)
            for t in range(4):
                lora(t)
            base(4)
            base(5)
            lora_transposed(1)
            base(6)
            pe.wait_ge(ht_lo, 2)
            lora(4)
            lora(5)
            lora(6)
            base(7)
            lora(7)


def decay_tables():
    f = np.float32
    base = f(1.0 / 2.0 ** (8.0 / HEADS))
    factor = f(1.0 - 1 / (32 - 1 + 1e-05) + 1e-05)
    slope = (base ** (np.arange(HEADS, dtype=f) + f(1)) * factor).astype(np.float64)
    d = np.arange(SEQ)[None, :] - np.arange(P)[:, None]
    table = np.where(d >= 0, np.exp(-slope[:, None, None] * np.maximum(d, 0)), 0.0).astype(f)
    table = np.concatenate([table, table[:, :, :P]], axis=2)
    return np.concatenate([table, table[:2]], axis=0)


def kernel(L0_attn_hidden_states, L0_attn_qkv_w, L0_attn_out_w, L0_attn_gate_w, L0_attn_norm_w, L0_ffn_base_W,
           L0_ffn_base_b, L0_ffn_router_W, L0_ffn_router_b, L0_ffn_A, L0_ffn_B, L0_ffn_expert_map):
    from concourse import bacc
    from concourse.bass_utils import run_bass_kernel_spmd

    x = np.ascontiguousarray(L0_attn_hidden_states).reshape(TOK, HID)
    qkv = np.asarray(L0_attn_qkv_w).reshape(HEADS, 3, P, KT, P)
    gate = np.asarray(L0_attn_gate_w).reshape(HEADS, P, KT, P)

    def per_head(w):
        return w.transpose(0, 3, 2, 1).reshape(HEADS, P, W)

    wq, wk, wg = per_head(qkv[:, 0]), per_head(qkv[:, 1]), per_head(gate)
    wv = qkv[:, 2].reshape(GROUPS, HG, P, KT, P).transpose(0, 3, 4, 1, 2).reshape(GROUPS, KT, P, W)
    wo = np.asarray(L0_attn_out_w).reshape(HID, HEADS, P).transpose(1, 2, 0)
    xt = x.reshape(2, W, KT, P).transpose(0, 2, 3, 1).reshape(XCH, P, W)
    chunks = []
    for g in range(GROUPS):
        place = {"q": 0, "k": 0, "g": 0, "v": 0, "o": 0}
        for kind in CHUNKS:
            n = place[kind]
            place[kind] += 1
            if kind == "v":
                chunks.append(wv[g, n])
            elif kind == "o":
                chunks.append(wo[HG * (g - 1) + n] if g else np.zeros_like(wo[0]))
            else:
                chunks.append({"q": wq, "k": wk, "g": wg}[kind][HG * g + n])
    chunks += list(wo[HEADS - HG:])
    chunks += list(np.asarray(L0_ffn_base_W).reshape(HID, KT, P).transpose(1, 2, 0))
    chunks.append(np.asarray(L0_ffn_A).reshape(NEXP * RANK, KT, P).transpose(2, 1, 0).reshape(P, W))
    chunks.append(np.asarray(L0_ffn_B).transpose(0, 2, 1).reshape(NEXP * RANK, HID))
    stream = np.stack(chunks[:1] + list(xt) + chunks[1:])
    router = np.zeros((P, KT, RANK), np.float32)
    router[:, :, :NROUTE] = np.asarray(L0_ffn_router_W).reshape(NROUTE, KT, P).transpose(2, 1, 0)
    fresh = np.ones((HG, NROUTE), np.float32)
    fresh[:, 0] = 0.0
    arrays = {
        "stream": stream, "x": x, "decay": decay_tables(),
        "norm_w": np.asarray(L0_attn_norm_w).reshape(HEADS, P).T,
        "base_b": np.asarray(L0_ffn_base_b), "router_w": router, "router_b": np.asarray(L0_ffn_router_b),
        "expert_map": np.asarray(L0_ffn_expert_map),
        "ident_in": np.eye(P, dtype=np.float32), "ones_in": np.ones((P, 2), np.float32), "fresh_in": fresh.reshape(-1),
    }
    arrays = {n: np.ascontiguousarray(a) for n, a in arrays.items()}
    nc = bacc.Bacc("TRN2", target_bir_lowering=False, num_devices=1, dynamic_dma_scratch_size=1024)
    args = {n: nc.dram_tensor(n, a.shape, mybir.dt.from_np(a.dtype), kind="ExternalInput").ap()
            for n, a in arrays.items()}
    out = nc.dram_tensor("out", (TOK, HID), FP32, kind="ExternalOutput").ap()
    build(nc, out=out, **args)
    r = run_bass_kernel_spmd(nc, [arrays], core_ids=[0])
    return r.results[0]["out"].reshape(L0_attn_hidden_states.shape)
```

```python
import numpy as np
import concourse.bass as bass
from concourse import mybir
from concourse.alu_op_type import AluOpType as ALU
from contextlib import ExitStack

FP32 = mybir.dt.float32
FP32R = mybir.dt.float32r
I32 = mybir.dt.int32
ACT = mybir.ActivationFunctionType
AX = mybir.AxisListType

P = 128
BATCH, SEQ, HID = 4, 256, 512
TOK = BATCH * SEQ
TT = TOK // P
HEADS, BLOCK = 32, 32
KT = HID // P
HG = 4
GROUPS = HEADS // HG
W = 512
SC = SEQ + P
NEXP, NROUTE, RANK = 8, 15, 16
AR = NEXP * RANK + 16
SCALING = 2.0
EPS = 1e-5

CHUNKS = (["q", "k", "v", "v", "v", "v", "g"] + ["q", "k", "o", "o", "o", "o", "g"]
          + ["q", "k", "g"] + ["q", "k", "g"])
NCH = len(CHUNKS)
QCH = [0, 7, 14, 17]
KCH = [1, 8, 15, 18]
GCH = [6, 13, 16, 19]
VCH, OCH = 2, 9
SPLITS = [range(first, gate + 1) for first, gate in zip((VCH, OCH, QCH[2], QCH[3]), GCH)]
AHEAD = 10
RAW = 5
XCH = 2 * KT
TAIL_OCH, BASECH, BCH = 0, 4, 8
CONSTS = 7
NSTREAM = GROUPS * NCH + AHEAD

PROJ = ["q"] * 2 + ["k"] * 2 + ["v"] * TT + ["g"] * 2 + (["q"] * 2 + ["k"] * 2 + ["g"] * 2) * 3
NPROJ = len(PROJ)
NSILU = sum(j != "g" for j in PROJ)
NGATE = NPROJ - NSILU
QJOB, KJOB, GJOB, VJOB = [0, 14, 20, 26], [2, 16, 22, 28], [12, 18, 24, 30], 4
WARMUP = 11
DVE_X = 3
TAIL_BANK = [4, 5, 2, 3, 0, 1, 6, 7]
FFN_BANK = [2, 3, 0, 1, 7, 2, 3, 0]


def silu_no(i):
    return sum(j != "g" for j in PROJ[:i])


def gate_no(i):
    return sum(j == "g" for j in PROJ[:i])


def build(nc, stream, xt, x, decay, norm_w, base_b, lora_router, router_b, expert_map, ident_in, ones_in, fresh_in, out):
    ctx = ExitStack()
    with ctx:
        def sb(name, shape, dt=FP32):
            return ctx.enter_context(nc.sbuf_tensor(name, shape, dt))

        def sem(name):
            return ctx.enter_context(nc.semaphore(name))

        raw = sb("raw", [P, RAW, W])
        wh = sb("wh", [P, AHEAD, W], FP32R)
        wl = sb("wl", [P, AHEAD, W], FP32R)
        xh = sb("xh", [P, KT, TOK], FP32R)
        xl = sb("xl", [P, KT, TOK], FP32R)
        q2 = sb("q2", [P, 2, TOK], FP32R)
        qh, ql = q2[:, 0, :], q2[:, 1, :]
        kh = sb("kh", [P, TOK], FP32R)
        kl = sb("kl", [P, TOK], FP32R)
        vh = sb("vh", [P, TT, W], FP32R)
        vl = sb("vl", [P, TT, W], FP32R)
        s2 = sb("s2", [P, 2, BATCH, SC], FP32R)
        sh, sl = s2[:, 0, :, :], s2[:, 1, :, :]
        yh = sb("yh", [P, HG, TOK], FP32R)
        yl = sb("yl", [P, HG, TOK], FP32R)
        sig = sb("sig", [P, 2, W])
        gate = sb("gate", [P, 2, W])
        sfull = sb("sfull", [P, 2, W])
        sq = sb("sq", [P, 2, W])
        bb = sq[:, 0, :]
        sqacc = sb("sqacc", [P, 2, W])
        acc = sb("acc", [P, TT, HID])
        dec = sb("dec", [P, 2, SEQ])
        nw = sb("nw", [P, HEADS])
        ident = sb("ident", [P, P])
        ones = sb("ones", [P, 2])
        ar = sb("ar", [P, KT, AR])
        arh = sb("arh", [P, KT, AR], FP32R)
        arl = sb("arl", [P, KT, AR], FP32R)
        rb = sb("rb", [P, NROUTE])
        emap = sb("emap", [P, NROUTE], I32)
        fresh = sb("fresh", [P, HG * NROUTE])
        route = sb("route", [P, NEXP, NROUTE])
        rms = sb("rms", [P, TT])
        meansq = sb("meansq", [P, TT])
        warm = sb("warm", [P, TT])
        half_power = sb("half_power", [P, TT])
        stat = sb("stat", [P, 2 * TT, 6])
        mv = sb("mv", [P, 2 * TT, 2])
        var_eps = sb("var_eps", [P, 2 * TT])
        neg_mean = sb("neg_mean", [P, 2 * TT])
        rstd = sb("rstd", [P, 2 * TT])
        shift = sb("shift", [P, 2 * TT])
        prob = sb("prob", [P, HG, NROUTE])
        red = sb("red", [P, HG])
        top = sb("top", [P, HG, NEXP])
        above = sb("above", [P, HG, NROUTE])
        equal = sb("equal", [P, HG, NROUTE])
        taken = sb("taken", [P, HG, NROUTE])
        wexp = sfull[:, :, :].rearrange("p a n -> p (a n)")[:, 0:HG * NEXP * NROUTE]\
            .rearrange("p (t e i) -> p t e i", t=HG, e=NEXP)
        wsum = sb("wsum", [P, HG, NEXP])
        hw = sig[:, 0, :].rearrange("p (t n) -> p t n", t=HG)
        ps = ctx.enter_context(nc.psum_tensor("ps", [P, 8, W], FP32))
        PROJ_B, S_B, AO_B = 0, 4, 6

        x_in = [sem(f"x_in{i}") for i in range(XCH)]
        zeros_set, x_hi, x_lo = sem("zeros_set"), sem("x_hi"), sem("x_lo")
        raw_in = [sem(f"raw_in{i}") for i in range(RAW)]
        bias_in = sem("bias_in")
        dec_in = [sem(f"dec_in{i}") for i in range(2)]
        const_in = sem("const_in")
        stored = [sem(f"stored{t}") for t in range(TT)]
        split_hi, split_lo = sem("split_hi"), sem("split_lo")
        ar_hi, ar_lo = sem("ar_hi"), sem("ar_lo")
        proj_done, sig_done, silu_full = sem("proj_done"), sem("sig_done"), sem("silu_full")
        silu_hi, silu_lo, gate_done = sem("silu_hi"), sem("silu_lo"), sem("gate_done")
        s_parts = sem("s_parts")
        s_done, s_full, s_hi, s_lo = sem("s_done"), sem("s_full"), sem("s_hi"), sem("s_lo")
        att_done, sq_done, sq_added = sem("att_done"), sem("sq_done"), sem("sq_added")
        att_part, att_full = sem("att_part"), sem("att_full")
        y_full, y_hi, y_lo = sem("y_full"), sem("y_hi"), sem("y_lo")
        o_done, o_added = sem("o_done"), sem("o_added")
        ss_done, meansq_done, rms_done, power_set = sem("ss_done"), sem("meansq_done"), sem("rms_done"), sem("power_set")
        acc_scaled, x_added, last_added, x1_done, stats_done = sem("acc_scaled"), sem("x_added"), sem("last_added"), sem("x1_done"), sem("stats_done")
        affine_done, ln1_done, bias_added = sem("affine_done"), sem("ln1_done"), sem("bias_added")
        pool_step = sem("pool_step")
        tr_done, tr_hi, tr_lo = sem("tr_done"), sem("tr_hi"), sem("tr_lo")
        hl_done, shifted, exp_done, hw_done = sem("hl_done"), sem("shifted"), sem("exp_done"), sem("hw_done")
        ht_done, ht_hi, ht_lo = sem("ht_done"), sem("ht_hi"), sem("ht_lo")
        ffn_done, ffn_read, out_ready = sem("ffn_done"), sem("ffn_read"), sem("out_ready")
        ffn_copied, ffn_added = sem("ffn_copied"), sem("ffn_added")
        dve_step = sem("dve_step")

        block = ctx.enter_context(nc.Block())

        def half(i):
            return slice(i * W, i * W + W)

        def tile(t):
            return slice(t * P, t * P + P)

        def att_banks(e, c0, c1):
            return ps[:, S_B + 2 * e:S_B + 2 * e + 2, c0:c1]

        def by_batch(ap):
            return ap.rearrange("p (b n) -> p b n", b=2)

        def f32(ap):
            return ap.bitcast(FP32)

        @block.sync
        def _(sp):
            def load(m):
                sp.dma_start(raw[:, m % RAW, :], stream[m]).then_inc(raw_in[m % RAW], 16)

            load(0)
            for c in range(XCH):
                sp.dma_start(acc[:, c, :], xt[c]).then_inc(x_in[c], 16)
            for m in range(1, RAW):
                load(m)
            for m in range(RAW, AHEAD):
                sp.wait_ge(split_lo, m - RAW + 1)
                load(m)
            for dst, src in ((nw[:, :], norm_w), (ident[:, :], ident_in), (ones[:, :], ones_in),
                             (rb[:, :], router_b.partition_broadcast(P)),
                             (emap[:, :], expert_map.partition_broadcast(P)), (ar[:, :, :], lora_router),
                             (fresh[:, :], fresh_in.partition_broadcast(P))):
                sp.dma_start(dst, src).then_inc(const_in, 16)
            with sp.Fori(0, GROUPS) as g:
                for j in range(NCH):
                    m0 = AHEAD + j
                    sp.wait_ge(split_lo, g * NCH + (m0 - RAW + 1))
                    src = stream[bass.ds(g * NCH + m0, 1), :, :].rearrange("a p n -> p (a n)")
                    sp.dma_start(raw[:, m0 % RAW, :], src).then_inc(raw_in[m0 % RAW], 16)
            for t in range(TT):
                m = NSTREAM + t
                if t == RAW:
                    sp.wait_ge(sq_added, 2 + 2 * HEADS)
                    sp.dma_start(bb, base_b.partition_broadcast(P)).then_inc(bias_in, 16)
                if t < RAW:
                    sp.wait_ge(split_lo, m - RAW + 1)
                else:
                    sp.wait_ge(x1_done, t - RAW + 1)
                sp.dma_start(raw[:, m % RAW, :], x[tile(t), :]).then_inc(raw_in[m % RAW], 16)
            for t in range(TT):
                sp.wait_ge(out_ready, t + 1)
                sp.dma_start(out[tile(t), :], acc[:, t, :]).then_inc(stored[t], 16)
            for t in range(TT):
                sp.wait_ge(stored[t], 16)

        def hl_bank(f, b):
            return ps[:, 6 - 2 * f + b, 0:2 * AR].rearrange("p (t n) -> p t n", t=2)

        def arrived(eng, g, m0):
            eng.wait_ge(raw_in[m0 % RAW], g * (16 * NCH // RAW) + 16 * (m0 // RAW + 1))

        @block.scalar
        def _(act):
            def load_decay(h, slot):
                src = decay[bass.ds(h, 1), :, :].rearrange("a p n -> p (a n)")
                act.dma_start(dec[:, slot, :], src).then_inc(dec_in[slot], 16)

            def split_chunk(g, u):
                arrived(act, g, AHEAD + u)
                s = CHUNKS[:u].count("g")
                if CHUNKS[u] != "o":
                    jobs = {"q": QJOB[s] + 2, "k": KJOB[s] + 2, "v": VJOB + TT, "g": GJOB[s] + 2}[CHUNKS[u]]
                    act.wait_ge(proj_done, g * NPROJ + jobs)
                elif not isinstance(g, int):
                    act.wait_ge(o_done, g * TT)
                nc.scalar.activation(wh[:, u % AHEAD, :], raw[:, (AHEAD + u) % RAW, :], ACT.Copy)\
                    .then_inc(split_hi, 1)

            def front(g, i):
                n = silu_no(i)
                act.wait_ge(proj_done, g * NPROJ + (i + 1))
                if n >= 2 or not isinstance(g, int):
                    act.wait_ge(silu_lo, g * NSILU + (n - 1))
                nc.scalar.activation(sig[:, n % 2, :], ps[:, PROJ_B + i % 4, :], ACT.Sigmoid).then_inc(sig_done, 1)

            def back(g, i, dst):
                n = silu_no(i)
                act.wait_ge(silu_full, g * NSILU + (n + 1))
                nc.scalar.activation(dst, sig[:, n % 2, :], ACT.Copy).then_inc(silu_hi, 1)

            def gate_half(g, s, e):
                i = GJOB[s] + e
                act.wait_ge(proj_done, g * NPROJ + (i + 1))
                if s > 0 or not isinstance(g, int):
                    act.wait_ge(y_lo, g * (2 * HG) + (2 * (s - 1) + e + 1))
                nc.scalar.activation(gate[:, e, :], ps[:, PROJ_B + i % 4, :], ACT.Sigmoid).then_inc(gate_done, 1)

            def scores(g, s, batches):
                for b in batches:
                    act.wait_ge(s_full, g * (HG * BATCH) + (s * BATCH + b + 1))
                    nc.scalar.activation(sh[:, b, :], sfull[:, b % 2, 0:SC], ACT.Copy).then_inc(s_hi, 1)

            def attention(g, s):
                r = (s - 1) % HG
                for e in range(2):
                    act.wait_ge(att_done, g * (2 * HG) + (2 * (s - 1) + e + 1))
                    nc.scalar.activation(by_batch(sfull[:, e, 0:SEQ]), att_banks(e, SEQ, SC), ACT.Copy)\
                        .then_inc(att_part, 1)
                for e in range(2):
                    a = 2 * (s - 1) + e
                    act.wait_ge(att_full, g * (2 * HG) + (a + 1))
                    if a >= 2 or not isinstance(g, int) or g > 0:
                        act.wait_ge(sq_added, g * (2 * HG) + (a + 1))
                    nc.scalar.activation(by_batch(sq[:, e, :]), att_banks(e, 0, SEQ), ACT.Square).then_inc(sq_done, 1)
                for e in range(2):
                    act.wait_ge(y_full, g * (2 * HG) + (2 * (s - 1) + e + 1))
                    nc.scalar.activation(yh[:, r, half(e)], gate[:, e, :], ACT.Copy).then_inc(y_hi, 1)

            def group(g, first):
                for s in range(HG):
                    q, k = QJOB[s], KJOB[s]
                    front(g, q)
                    front(g, q + 1)
                    back(g, q, qh[:, half(0)])
                    front(g, k)
                    back(g, q + 1, qh[:, half(1)])
                    front(g, k + 1)
                    back(g, k, kh[:, half(0)])
                    back(g, k + 1, kh[:, half(1)])
                    if s == 0 and first:
                        for m in range(GCH[0], AHEAD):
                            split_first(m)
                    if s < 2:
                        split_chunk(g, QCH[s])
                        split_chunk(g, KCH[s])
                    if s > 0 or not first:
                        attention(g, s)
                    if s == 0:
                        for t in range(TT):
                            front(g, VJOB + t)
                            if t:
                                back(g, VJOB + t - 1, vh[:, t - 1, :])
                        back(g, VJOB + TT - 1, vh[:, TT - 1, :])
                    gate_half(g, s, 0)
                    gate_half(g, s, 1)
                    scores(g, s, range(BATCH))
                    load_decay(g * HG + (s + 2), s % 2)
                    for u in SPLITS[s]:
                        split_chunk(g, u)

            act.wait_ge(power_set, 1)
            nc.scalar.activation(warm[:, :], half_power[:, :], ACT.Sigmoid)

            def split_first(m):
                arrived(act, 0, m)
                nc.scalar.activation(wh[:, m, :], raw[:, m % RAW, :], ACT.Copy).then_inc(split_hi, 1)

            split_first(0)
            for c in range(XCH):
                act.wait_ge(x_in[c], 16)
                nc.scalar.activation(xh[:, c % KT, half(c // KT)], acc[:, c, :], ACT.Copy).then_inc(x_hi, 1)
            load_decay(0, 0)
            load_decay(1, 1)
            for m in range(1, GCH[0]):
                split_first(m)
            group(0, True)
            with act.Fori(1, GROUPS) as g:
                group(g, False)
            attention(GROUPS, 0)

            def scale_acc(t):
                nc.scalar.activation(acc[:, t, :], acc[:, t, :], ACT.Copy, scale=rms[:, t:t + 1]).then_inc(acc_scaled, 1)

            def normalize(n, done):
                act.wait_ge(affine_done, n + 1)
                nc.scalar.activation(acc[:, n % TT, :], acc[:, n % TT, :], ACT.Identity, scale=rstd[:, n:n + 1],
                                     bias=shift[:, n:n + 1]).then_inc(done, 1)

            def transposed(t):
                act.wait_ge(tr_done, t + 1)
                nc.scalar.activation(xh[:, :, tile(t)], ps[:, 4 + t % 2, :].rearrange("p (k n) -> p k n", k=KT),
                                     ACT.Copy).then_inc(tr_hi, 1)

            def exponent(f):
                act.wait_ge(shifted, f + 1)
                nc.scalar.activation(prob[:, :, :], prob[:, :, :], ACT.Exp).then_inc(exp_done, 1)

            def lora_transposed(f):
                act.wait_ge(ht_done, f + 1)
                nc.scalar.activation(qh[:, half(f)], ps[:, 6, :], ACT.Copy).then_inc(ht_hi, 1)

            def copy_ffn(t):
                act.wait_ge(ffn_done, t + 1)
                nc.scalar.activation(raw[:, t, :], ps[:, FFN_BANK[t], :], ACT.Copy).then_inc(ffn_copied, 1)

            nc.scalar.activation(arh[:, :, :], ar[:, :, :], ACT.Copy).then_inc(ar_hi, 1)
            act.wait_ge(rms_done, 1)
            act.wait_ge(o_added, GROUPS * TT)
            for t in range(DVE_X, TT):
                scale_acc(t)
            normalize(0, ln1_done)
            normalize(1, ln1_done)
            transposed(0)
            transposed(1)
            normalize(2, ln1_done)
            normalize(3, ln1_done)
            transposed(2)
            transposed(3)
            normalize(4, ln1_done)
            normalize(5, ln1_done)
            transposed(4)
            transposed(5)
            normalize(6, ln1_done)
            normalize(7, ln1_done)
            transposed(6)
            transposed(7)
            exponent(0)
            lora_transposed(0)
            exponent(1)
            for t in range(4):
                copy_ffn(t)
            lora_transposed(1)
            for t in range(TT):
                normalize(TT + t, out_ready)
            for i in range(2):
                act.wait_ge(dec_in[i], 16 * (HEADS // 2 + 1))

        @block.vector
        def _(dve):
            def minus(dst, full, hi):
                return nc.vector.tensor_tensor(dst, full, f32(hi), ALU.subtract)

            def split_chunk(g, u):
                dve.wait_ge(split_hi, g * NCH + (AHEAD + u + 1))
                minus(wl[:, u % AHEAD, :], raw[:, (AHEAD + u) % RAW, :], wh[:, u % AHEAD, :])\
                    .then_inc(split_lo, 1)

            def front(g, i):
                n = silu_no(i)
                dve.wait_ge(sig_done, g * NSILU + (n + 1))
                nc.vector.tensor_tensor(sig[:, n % 2, :], ps[:, PROJ_B + i % 4, :], sig[:, n % 2, :], ALU.mult)\
                    .then_inc(silu_full, 1)

            def back(g, i, hi, lo):
                n = silu_no(i)
                dve.wait_ge(silu_hi, g * NSILU + (n + 1))
                minus(lo, sig[:, n % 2, :], hi).then_inc(silu_lo, 1)

            def mask(g, s, b):
                n = s * BATCH + b
                if n >= 2 or not isinstance(g, int):
                    dve.wait_ge(s_lo, g * (HG * BATCH) + (n - 1))
                dve.wait_ge(s_done, g * (HG * BATCH) + (n + 1))
                full, part = sfull[:, b % 2, :], ps[:, S_B + b, :]
                nc.vector.tensor_tensor(full[:, SEQ:W].rearrange("p (a n) -> p a n", a=2),
                                        part[:, SEQ:W].rearrange("p (a n) -> p a n", a=2),
                                        dec[:, s % 2, 0:P].unsqueeze(1).broadcast_to([P, 2, P]), ALU.mult)
                nc.vector.tensor_tensor(full[:, 0:SEQ], part[:, 0:SEQ], dec[:, s % 2, :], ALU.mult)\
                    .then_inc(s_parts, 1)
                dve.wait_ge(s_parts, g * (HG * BATCH) + (n + 1))
                nc.vector.tensor_tensor(full[:, SEQ:SC], full[:, SEQ:SC], full[:, SC:W], ALU.add).then_inc(s_full, 1)

            def scores_lo(g, s, b):
                dve.wait_ge(s_hi, g * (HG * BATCH) + (s * BATCH + b + 1))
                minus(sl[:, b, :], sfull[:, b % 2, 0:SC], sh[:, b, :]).then_inc(s_lo, 1)

            def scores(g, s):
                dve.wait_ge(dec_in[s % 2], g * (16 * HG // 2) + 16 * (s // 2 + 1))
                if s > 0 or not isinstance(g, int):
                    dve.wait_ge(att_full, g * (2 * HG) + 2 * s)
                for b in (0, 2):
                    mask(g, s, b)
                    mask(g, s, b + 1)
                    scores_lo(g, s, b)
                    scores_lo(g, s, b + 1)

            def attention(g, s):
                r = (s - 1) % HG
                for e in range(2):
                    dve.wait_ge(att_part, g * (2 * HG) + (2 * (s - 1) + e + 1))
                    nc.vector.tensor_tensor(att_banks(e, P, SEQ), att_banks(e, P, SEQ), by_batch(sfull[:, e, 0:SEQ]),
                                            ALU.add).then_inc(att_full, 1)
                for e in range(2):
                    a = 2 * (s - 1) + e
                    dve.wait_ge(sq_done, g * (2 * HG) + (a + 1))
                    dve.wait_ge(gate_done, g * NGATE + (a + 1))
                    h = g * HG + (s - 1)
                    scale = nw[:, h:h + 1] if isinstance(h, int) else nw[:, bass.ds(h, 1)]
                    nc.vector.scalar_tensor_tensor(out=by_batch(gate[:, e, :]), in0=att_banks(e, 0, SEQ), scalar=scale,
                                                   in1=by_batch(gate[:, e, :]), op0=ALU.mult, op1=ALU.mult)\
                        .then_inc(y_full, 1)
                for e in range(2):
                    a = 2 * (s - 1) + e
                    dve.wait_ge(sq_added, g * (2 * HG) + (a + 1))
                    nc.vector.tensor_tensor(sqacc[:, e, :], sqacc[:, e, :], sq[:, e, :], ALU.add)\
                        .then_inc(sq_added, 1)
                    dve.wait_ge(y_hi, g * (2 * HG) + (a + 1))
                    minus(yl[:, r, half(e)], gate[:, e, :], yh[:, r, half(e)]).then_inc(y_lo, 1)

            def output(g, t):
                dve.wait_ge(o_done, g * TT + (t - TT + 1))
                dve.wait_ge(o_added, g * TT + (t + 1 - TT))
                nc.vector.tensor_tensor(acc[:, t, :], acc[:, t, :], ps[:, AO_B + t % 2, :], ALU.add)\
                    .then_inc(o_added, 1)

            def group(g, first):
                for s in range(HG):
                    q, k = QJOB[s], KJOB[s]
                    front(g, q)
                    front(g, q + 1)
                    back(g, q, qh[:, half(0)], ql[:, half(0)])
                    front(g, k)
                    back(g, q + 1, qh[:, half(1)], ql[:, half(1)])
                    front(g, k + 1)
                    back(g, k, kh[:, half(0)], kl[:, half(0)])
                    back(g, k + 1, kh[:, half(1)], kl[:, half(1)])
                    if s == 0 and first:
                        for m in range(GCH[0], AHEAD):
                            split_first(m)
                    if s == 1 and not first:
                        output(g, 0)
                        output(g, 1)
                    if s < 2:
                        split_chunk(g, QCH[s])
                        split_chunk(g, KCH[s])
                    if s == 1 and not first:
                        for t in range(2, TT):
                            output(g, t)
                    if s == 1 and first:
                        dve.wait_ge(const_in, CONSTS * 16)
                    if s > 0 or not first:
                        attention(g, s)
                    if s == 0:
                        for t in range(TT):
                            front(g, VJOB + t)
                            if t:
                                back(g, VJOB + t - 1, vh[:, t - 1, :], vl[:, t - 1, :])
                        back(g, VJOB + TT - 1, vh[:, TT - 1, :], vl[:, TT - 1, :])
                    scores(g, s)
                    for u in SPLITS[s]:
                        split_chunk(g, u)

            def split_first(m):
                dve.wait_ge(split_hi, m + 1)
                minus(wl[:, m, :], raw[:, m % RAW, :], wh[:, m, :]).then_inc(split_lo, 1)

            nc.vector.memset(f32(sh[:, 0, :]), 0.0).then_inc(zeros_set, 1)
            split_first(0)
            for c in range(XCH):
                dve.wait_ge(x_hi, c + 1)
                minus(xl[:, c % KT, half(c // KT)], acc[:, c, :], xh[:, c % KT, half(c // KT)]).then_inc(x_lo, 1)
            for m in range(1, GCH[0]):
                split_first(m)
            group(0, True)
            with dve.Fori(1, GROUPS) as g:
                group(g, False)
            attention(GROUPS, 0)

            steps = [0]

            dve.wait_ge(ar_hi, 1)
            minus(arl[:, :, :], ar[:, :, :], arh[:, :, :]).then_inc(ar_lo, 1)

            def link(ins):
                steps[0] += 1
                ins.then_inc(dve_step, 1)
                dve.wait_ge(dve_step, steps[0])

            def moments(n):
                link(nc.vector.bn_stats(stat[:, n, :], acc[:, n % TT, :]))
                nc.vector.bn_aggr(mv[:, n, :], stat[:, n, :]).then_inc(stats_done, 1)

            def first_residual(t):
                if t < DVE_X:
                    dve.wait_ge(last_added, t + 1)
                    arrived(dve, 0, NSTREAM + t)
                    nc.vector.scalar_tensor_tensor(out=acc[:, t, :], in0=acc[:, t, :], scalar=rms[:, t:t + 1],
                                                   in1=raw[:, (NSTREAM + t) % RAW, :], op0=ALU.mult, op1=ALU.add)\
                        .then_inc(x1_done, 1)
                else:
                    dve.wait_ge(o_done, (GROUPS - 1) * TT + t + 1)
                    dve.wait_ge(x_added, t + 1 - DVE_X)
                    nc.vector.scalar_tensor_tensor(out=acc[:, t, :], in0=ps[:, TAIL_BANK[t], :],
                                                   scalar=rms[:, t:t + 1], in1=acc[:, t, :],
                                                   op0=ALU.mult, op1=ALU.add).then_inc(x1_done, 1)
                dve.wait_ge(x1_done, t + 1)
                moments(t)

            def transposed(t):
                dve.wait_ge(tr_hi, t + 1)
                minus(xl[:, :, tile(t)], ps[:, 4 + t % 2, :].rearrange("p (k n) -> p k n", k=KT),
                      xh[:, :, tile(t)]).then_inc(tr_lo, 1)

            def router(f):
                dve.wait_ge(hl_done, f + 1)
                each = [P, HG, NROUTE]
                for b in range(2):
                    lg = hl_bank(f, b)[:, :, NEXP * RANK:NEXP * RANK + NROUTE]
                    link(nc.vector.tensor_tensor(prob[:, 2 * b:2 * b + 2, :], lg,
                                                 rb[:, :].unsqueeze(1).broadcast_to([P, 2, NROUTE]), ALU.add))
                link(nc.vector.tensor_reduce(red[:, :], prob[:, :, :], AX.X, ALU.max))
                nc.vector.tensor_tensor(prob[:, :, :], prob[:, :, :], red[:, :].unsqueeze(2).broadcast_to(each),
                                        ALU.subtract).then_inc(shifted, 1)
                dve.wait_ge(exp_done, f + 1)
                link(nc.vector.tensor_reduce(red[:, :], prob[:, :, :], AX.X, ALU.add))
                link(nc.vector.reciprocal(red[:, :], red[:, :]))
                link(nc.vector.tensor_tensor(prob[:, :, :], prob[:, :, :],
                                             red[:, :].unsqueeze(2).broadcast_to(each), ALU.mult))
                for q in range(HG):
                    link(nc.vector.max(top[:, q, :], prob[:, q, :]))
                eighth = top[:, :, NEXP - 1:NEXP].broadcast_to(each)
                link(nc.vector.tensor_tensor(above[:, :, :], prob[:, :, :], eighth, ALU.is_gt))
                link(nc.vector.tensor_tensor(equal[:, :, :], prob[:, :, :], eighth, ALU.is_equal))
                link(nc.vector.tensor_reduce(red[:, :], above[:, :, :], AX.X, ALU.add))
                link(nc.vector.tensor_tensor_scan(taken[:, :, :].rearrange("p t n -> p (t n)"), fresh[:, :],
                                                  equal[:, :, :].rearrange("p t n -> p (t n)"), 0.0,
                                                  ALU.mult, ALU.add))
                link(nc.vector.tensor_tensor(taken[:, :, :], taken[:, :, :],
                                             red[:, :].unsqueeze(2).broadcast_to(each), ALU.add))
                link(nc.vector.scalar_tensor_tensor(out=equal[:, :, :], in0=taken[:, :, :], scalar=float(NEXP),
                                                    in1=equal[:, :, :], op0=ALU.is_le, op1=ALU.mult))
                link(nc.vector.tensor_tensor(above[:, :, :], above[:, :, :], equal[:, :, :], ALU.add))
                link(nc.vector.tensor_tensor(prob[:, :, :], prob[:, :, :], above[:, :, :], ALU.mult))
                link(nc.vector.tensor_tensor(wexp[:, :, :, :],
                                             prob[:, :, :].unsqueeze(2).broadcast_to([P, HG, NEXP, NROUTE]),
                                             route[:, :, :].unsqueeze(1).broadcast_to([P, HG, NEXP, NROUTE]), ALU.mult))
                link(nc.vector.tensor_reduce(wsum[:, :, :], wexp[:, :, :, :], AX.X, ALU.add))
                for b in range(2):
                    two = slice(2 * b, 2 * b + 2)
                    nc.vector.tensor_tensor(
                        hw[:, two, :].rearrange("p t (e r) -> p t e r", e=NEXP),
                        hl_bank(f, b)[:, :, 0:NEXP * RANK].rearrange("p t (e r) -> p t e r", e=NEXP),
                        wsum[:, two, :].unsqueeze(3).broadcast_to([P, 2, NEXP, RANK]), ALU.mult).then_inc(hw_done, 1)

            def lora_transposed(f):
                dve.wait_ge(ht_hi, f + 1)
                minus(ql[:, half(f)], ps[:, 6, :], qh[:, half(f)]).then_inc(ht_lo, 1)

            def second_residual(t):
                dve.wait_ge(ffn_done, t + 1)
                dve.wait_ge(bias_added, t + 1)
                nc.vector.tensor_tensor(acc[:, t, :], acc[:, t, :], ps[:, FFN_BANK[t], :], ALU.add).then_inc(ffn_read, 1)

            def second_moments(t):
                if t < 4:
                    dve.wait_ge(ffn_added, t + 1)
                else:
                    dve.wait_ge(ffn_read, t - 3)
                moments(TT + t)

            for e in range(NEXP):
                link(nc.vector.tensor_scalar(route[:, e, :], emap[:, :], float(e), SCALING, ALU.is_equal, ALU.mult))
            dve.wait_ge(ss_done, 1)
            nc.vector.tensor_scalar(meansq[:, :], ps[:, 7, 0:TT], 1.0 / (HEADS * P), EPS, ALU.mult, ALU.add)\
                .then_inc(meansq_done, 1)
            for t in range(DVE_X):
                dve.wait_ge(o_done, (GROUPS - 1) * TT + t + 1)
                dve.wait_ge(o_added, GROUPS * TT)
                nc.vector.tensor_tensor(acc[:, t, :], acc[:, t, :], ps[:, TAIL_BANK[t], :], ALU.add)\
                    .then_inc(last_added, 1)
            dve.wait_ge(rms_done, 1)
            for t in range(4):
                first_residual(t)
            transposed(0)
            transposed(1)
            first_residual(4)
            first_residual(5)
            transposed(2)
            transposed(3)
            first_residual(6)
            first_residual(7)
            for t in range(4, TT):
                transposed(t)
            router(0)
            lora_transposed(0)
            router(1)
            second_moments(0)
            lora_transposed(1)
            for t in range(1, 4):
                second_moments(t)
            for t in range(4, TT):
                second_residual(t)
                second_moments(t)

        @block.gpsimd
        def _(pool):
            steps = [0]

            def link(ins):
                steps[0] += 1
                ins.then_inc(pool_step, 1)
                pool.wait_ge(pool_step, steps[0])

            def affine(n):
                pool.wait_ge(stats_done, n + 1)
                nc.gpsimd.tensor_scalar(neg_mean[:, n:n + 1], mv[:, n, 0:1], -1.0, None, ALU.mult)
                link(nc.gpsimd.tensor_scalar(var_eps[:, n:n + 1], mv[:, n, 1:2], EPS, None, ALU.add))
                link(nc.gpsimd.tensor_tensor(rstd[:, n:n + 1], var_eps[:, n:n + 1], half_power[:, 0:1], ALU.pow))
                nc.gpsimd.tensor_tensor(shift[:, n:n + 1], neg_mean[:, n:n + 1], rstd[:, n:n + 1], ALU.mult)\
                    .then_inc(affine_done, 1)

            def add_x(t):
                m = NSTREAM + t
                pool.wait_ge(acc_scaled, t + 1 - DVE_X)
                arrived(pool, 0, m)
                nc.gpsimd.tensor_tensor(acc[:, t, :], acc[:, t, :], raw[:, m % RAW, :], ALU.add).then_inc(x_added, 1)

            def add_bias(t):
                pool.wait_ge(bias_in, 16)
                pool.wait_ge(tr_done, t + 1)
                nc.gpsimd.tensor_tensor(acc[:, t, :], acc[:, t, :], bb, ALU.add).then_inc(bias_added, 1)

            nc.gpsimd.memset(half_power[:, :], -0.5).then_inc(power_set, 1)
            nc.gpsimd.memset(sqacc[:, :, :], 0.0).then_inc(sq_added, 2)
            pool.wait_ge(x_lo, XCH)
            nc.gpsimd.memset(acc[:, :, :], 0.0).then_inc(o_added, TT)
            pool.wait_ge(power_set, 1)
            pool.wait_ge(const_in, CONSTS * 16)
            pool.wait_ge(meansq_done, 1)
            nc.gpsimd.tensor_tensor(rms[:, :], meansq[:, :], half_power[:, :], ALU.pow).then_inc(rms_done, 1)
            add_x(3)
            for t in range(TT):
                affine(t)
                if t + 4 < TT:
                    add_x(t + 4)
            for t in range(TT):
                add_bias(t)
            for t in range(4):
                pool.wait_ge(ffn_copied, t + 1)
                pool.wait_ge(bias_added, t + 1)
                nc.gpsimd.tensor_tensor(acc[:, t, :], acc[:, t, :], raw[:, t, :], ALU.add).then_inc(ffn_added, 1)
            for t in range(TT):
                affine(TT + t)

        @block.tensor
        def _(pe):
            def mm3(dst, wt, mv_, start, stop):
                nc.tensor.matmul(dst, wt[0], mv_[0], start=start, stop=False)
                nc.tensor.matmul(dst, wt[0], mv_[1], start=False, stop=False)
                return nc.tensor.matmul(dst, wt[1], mv_[0], start=False, stop=stop)

            def chunk_ready(g, n):
                pe.wait_ge(split_lo, g * NCH + (n + 1))

            def bank_free(g, i):
                j, back = (i - 4, 0) if i >= 4 else (i - 4 + NPROJ, 1)
                if back and isinstance(g, int):
                    return
                if PROJ[j] == "g":
                    pe.wait_ge(gate_done, g * NGATE + (gate_no(j) + 1 - back * NGATE))
                else:
                    pe.wait_ge(silu_full, g * NSILU + (silu_no(j) + 1 - back * NSILU))

            def project(g, i, c, e, ready=None):
                bank_free(g, i)
                r = c % AHEAD
                for k in range(KT):
                    if ready is not None:
                        ready(k)
                    last = mm3(ps[:, PROJ_B + i % 4, :], (wh[:, r, tile(k)], wl[:, r, tile(k)]),
                               (xh[:, k, half(e)], xl[:, k, half(e)]), k == 0, k == KT - 1)
                last.then_inc(proj_done, 1)

            def first_projection():
                bank = ps[:, PROJ_B, :]
                pe.wait_ge(split_hi, 1)
                for k in range(KT):
                    pe.wait_ge(x_hi, k + 1)
                    nc.tensor.matmul(bank, wh[:, 0, tile(k)], xh[:, k, half(0)], start=k == 0, stop=False)
                    if k == 0:
                        pe.wait_ge(split_lo, 1)
                    nc.tensor.matmul(bank, wl[:, 0, tile(k)], xh[:, k, half(0)], start=False, stop=False)
                for k in range(KT):
                    pe.wait_ge(x_lo, k + 1)
                    last = nc.tensor.matmul(bank, wh[:, 0, tile(k)], xl[:, k, half(0)], start=False, stop=k == KT - 1)
                last.then_inc(proj_done, 1)

            def both_halves(g, i, c):
                chunk_ready(g, c)
                project(g, i, c, 0)
                project(g, i + 1, c, 1)

            def values(g):
                for k in range(KT):
                    chunk_ready(g, VCH + k)
                for t in range(TT):
                    i = VJOB + t
                    bank_free(g, i)
                    for k in range(KT):
                        r = (VCH + k) % AHEAD
                        last = mm3(ps[:, PROJ_B + i % 4, :], (xh[:, k, tile(t)], xl[:, k, tile(t)]),
                                   (wh[:, r, :], wl[:, r, :]), k == 0, k == KT - 1)
                    last.then_inc(proj_done, 1)

            def scores(g, s, batches):
                pe.wait_ge(silu_lo, g * NSILU + (silu_no(KJOB[s] + 1) + 1))
                for b in batches:
                    if b % 2 == 0 and (s > 0 or not isinstance(g, int)):
                        pe.wait_ge(y_full, g * (2 * HG) + (2 * (s - 1) + b // 2 + 1))
                    q0 = b * SEQ
                    mm3(ps[:, S_B + b, 0:SEQ], (kh[:, q0:q0 + P], kl[:, q0:q0 + P]),
                        (qh[:, q0:q0 + SEQ], ql[:, q0:q0 + SEQ]), True, True)
                    nc.tensor.matmul(ps[:, S_B + b, SEQ:W], kh[:, q0 + P:q0 + SEQ], q2[:, :, q0 + P:q0 + SEQ],
                                     start=True, stop=False)
                    nc.tensor.matmul(ps[:, S_B + b, SEQ:SC], kl[:, q0 + P:q0 + SEQ], qh[:, q0 + P:q0 + SEQ],
                                     start=False, stop=True).then_inc(s_done, 1)

            def attention(g, s):
                r = (s - 1) % HG
                hs = slice(r * P, r * P + P)
                if s == 1:
                    pe.wait_ge(silu_lo, g * NSILU + (silu_no(VJOB + TT - 1) + 1))
                pe.wait_ge(s_lo, g * (HG * BATCH) + s * BATCH)
                for e in range(2):
                    if e and s == 1 and not isinstance(g, int):
                        pe.wait_ge(o_added, g * TT + TT)
                    for b in (2 * e, 2 * e + 1):
                        bank = ps[:, S_B + b, :]
                        mm3(bank[:, 0:SEQ], (vh[:, 2 * b, hs], vl[:, 2 * b, hs]),
                            (sh[:, b, 0:SEQ], sl[:, b, 0:SEQ]), True, False)
                        nc.tensor.matmul(bank[:, P:SC], vh[:, 2 * b + 1, hs], s2[:, :, b, SEQ:SC],
                                         start=False, stop=False, skip_group_check=True)
                        last = nc.tensor.matmul(bank[:, P:SEQ], vl[:, 2 * b + 1, hs], sh[:, b, SEQ:SC],
                                                start=False, stop=True)
                    last.then_inc(att_done, 1)

            def output(g, t):
                if t < 2:
                    pe.wait_ge(y_lo, g * (2 * HG))
                else:
                    pe.wait_ge(o_added, g * TT + (t - 1))
                for hh in range(HG):
                    r = (OCH + hh) % AHEAD
                    last = mm3(ps[:, AO_B + t % 2, :], (yh[:, hh, tile(t)], yl[:, hh, tile(t)]),
                               (wh[:, r, :], wl[:, r, :]), hh == 0, hh == HG - 1)
                last.then_inc(o_done, 1)

            def group(g, first):
                for s in range(HG):
                    if s == 0 and first:
                        first_projection()
                        project(g, 1, 0, 1, ready=lambda k: pe.wait_ge(x_lo, KT + k + 1))
                    else:
                        both_halves(g, QJOB[s], QCH[s])
                    both_halves(g, KJOB[s], KCH[s])
                    if s == 1 and not first:
                        chunk_ready(g, OCH + HG - 1)
                        pe.wait_ge(s_full, g * (HG * BATCH) + BATCH)
                        for t in range(TT):
                            output(g, t)
                    if s > 0 or not first:
                        attention(g, s)
                    if s == 0:
                        values(g)
                    chunk_ready(g, GCH[s])
                    project(g, GJOB[s], GCH[s], 0)
                    project(g, GJOB[s] + 1, GCH[s], 1)
                    scores(g, s, range(BATCH))

            pe.wait_ge(zeros_set, 1)
            for _ in range(WARMUP):
                nc.tensor.matmul(ps[:, 7, 0:SC], sh[:, 0, 0:P], sh[:, 0, :], start=True, stop=True)
            group(0, True)
            with pe.Fori(1, GROUPS) as g:
                group(g, False)

            def tail_output(t, heads):
                for hh in heads:
                    last = mm3(ps[:, TAIL_BANK[t], :], (yh[:, hh, tile(t)], yl[:, hh, tile(t)]),
                               (wh[:, TAIL_OCH + hh, :], wl[:, TAIL_OCH + hh, :]), hh == 0, hh == HG - 1)
                return last

            def sum_of_squares():
                pe.wait_ge(sq_added, 2 + 2 * HEADS)
                pe.wait_ge(y_full, 2 * HEADS)
                for t in range(TT):
                    last = nc.tensor.matmul(ps[:, 7, t:t + 1], sqacc[:, t // 4, tile(t % 4)], ones[:, 0:1],
                                            start=True, stop=True)
                last.then_inc(ss_done, 1)

            def transposed(t):
                pe.wait_ge(ln1_done, t + 1)
                if t >= 2:
                    pe.wait_ge(tr_lo, t - 1)
                for k in range(KT):
                    last = nc.tensor.transpose(ps[:, 4 + t % 2, tile(k)], acc[:, t, tile(k)], ident[:, :])
                last.then_inc(tr_done, 1)

            def router_and_lora(f):
                if f:
                    pe.wait_ge(tr_lo, TT)
                else:
                    pe.wait_ge(x1_done, TT)
                for q in range(4):
                    t = 4 * f + q
                    pe.wait_ge(tr_lo, t + 1)
                    for k in range(KT):
                        last = mm3(hl_bank(f, q // 2)[:, q % 2, :], (xh[:, k, tile(t)], xl[:, k, tile(t)]),
                                   (arh[:, k, :], arl[:, k, :]), k == 0, k == KT - 1)
                last.then_inc(hl_done, 1)

            def base(t):
                pe.wait_ge(tr_lo, t + 1)
                if t < 4:
                    pe.wait_ge(x1_done, t + 3)
                elif t == 4:
                    pe.wait_ge(hw_done, 2)
                else:
                    pe.wait_ge(ffn_copied, t - 4)
                for k in range(KT):
                    mm3(ps[:, FFN_BANK[t], :], (xh[:, k, tile(t)], xl[:, k, tile(t)]),
                        (wh[:, BASECH + k, :], wl[:, BASECH + k, :]), k == 0, False)

            def lora(t):
                mm3(ps[:, FFN_BANK[t], :], (qh[:, tile(t)], ql[:, tile(t)]), (wh[:, BCH, :], wl[:, BCH, :]),
                    False, True).then_inc(ffn_done, 1)

            def lora_transposed(f):
                pe.wait_ge(hw_done, 2 * f + 2)
                for q in range(4):
                    last = nc.tensor.transpose(ps[:, 6, tile(q)], hw[:, q, :], ident[:, :])
                last.then_inc(ht_done, 1)

            pe.wait_ge(y_lo, 2 * (HEADS - 1))
            chunk_ready(GROUPS, TAIL_OCH + HG - 1)
            pe.wait_ge(silu_full, GROUPS * NSILU)
            first_heads = range(HG - 1)
            tail_output(4, first_heads)
            tail_output(5, first_heads)
            pe.wait_ge(gate_done, GROUPS * NGATE)
            tail_output(2, first_heads)
            attention(GROUPS, 0)
            tail_output(3, first_heads)
            pe.wait_ge(y_full, 2 * HEADS - 1)
            tail_output(0, first_heads)
            sum_of_squares()
            tail_output(1, first_heads)
            pe.wait_ge(y_lo, 2 * HEADS)
            for t in range(6):
                tail_output(t, [HG - 1]).then_inc(o_done, 1)
            pe.wait_ge(meansq_done, 1)
            tail_output(6, range(HG)).then_inc(o_done, 1)
            transposed(0)
            tail_output(7, range(HG)).then_inc(o_done, 1)
            transposed(1)
            pe.wait_ge(ar_lo, 1)
            chunk_ready(GROUPS, BCH)
            base(0)
            transposed(2)
            transposed(3)
            base(1)
            transposed(4)
            transposed(5)
            base(2)
            transposed(6)
            transposed(7)
            router_and_lora(0)
            base(3)
            router_and_lora(1)
            lora_transposed(0)
            base(4)
            pe.wait_ge(ht_lo, 1)
            for t in range(4):
                lora(t)
            base(5)
            lora_transposed(1)
            base(6)
            pe.wait_ge(ht_lo, 2)
            lora(4)
            lora(5)
            lora(6)
            base(7)
            lora(7)


def decay_tables():
    f = np.float32
    base = f(1.0 / 2.0 ** (8.0 / HEADS))
    factor = f(1.0 - 1 / (32 - 1 + 1e-05) + 1e-05)
    slope = (base ** (np.arange(HEADS, dtype=f) + f(1)) * factor).astype(np.float64)
    d = np.arange(SEQ)[None, :] - np.arange(P)[:, None]
    table = np.where(d >= 0, np.exp(-slope[:, None, None] * np.maximum(d, 0)), 0.0).astype(f)
    return np.concatenate([table, table[:2]], axis=0)


def kernel(L0_attn_hidden_states, L0_attn_qkv_w, L0_attn_out_w, L0_attn_gate_w, L0_attn_norm_w, L0_ffn_base_W,
           L0_ffn_base_b, L0_ffn_router_W, L0_ffn_router_b, L0_ffn_A, L0_ffn_B, L0_ffn_expert_map):
    from concourse import bacc
    from concourse.bass_utils import run_bass_kernel_spmd

    x = np.ascontiguousarray(L0_attn_hidden_states).reshape(TOK, HID)
    qkv = np.asarray(L0_attn_qkv_w).reshape(HEADS, 3, P, KT, P)
    gate = np.asarray(L0_attn_gate_w).reshape(HEADS, P, KT, P)

    def per_head(w):
        return w.transpose(0, 3, 2, 1).reshape(HEADS, P, W)

    wq, wk, wg = per_head(qkv[:, 0]), per_head(qkv[:, 1]), per_head(gate)
    wv = qkv[:, 2].reshape(GROUPS, HG, P, KT, P).transpose(0, 3, 4, 1, 2).reshape(GROUPS, KT, P, W)
    wo = np.asarray(L0_attn_out_w).reshape(HID, HEADS, P).transpose(1, 2, 0)
    xt = x.reshape(2, W, KT, P).transpose(0, 2, 3, 1).reshape(XCH, P, W)
    chunks = []
    for g in range(GROUPS):
        place = {"q": 0, "k": 0, "g": 0, "v": 0, "o": 0}
        for kind in CHUNKS:
            n = place[kind]
            place[kind] += 1
            if kind == "v":
                chunks.append(wv[g, n])
            elif kind == "o":
                chunks.append(wo[HG * (g - 1) + n] if g else np.zeros_like(wo[0]))
            else:
                chunks.append({"q": wq, "k": wk, "g": wg}[kind][HG * g + n])
    chunks += list(wo[HEADS - HG:])
    chunks += list(np.asarray(L0_ffn_base_W).reshape(HID, KT, P).transpose(1, 2, 0))
    chunks.append(np.asarray(L0_ffn_B).transpose(0, 2, 1).reshape(NEXP * RANK, HID))
    chunks.append(np.zeros_like(wo[0]))
    lora_router = np.zeros((P, KT, AR), np.float32)
    lora_router[:, :, :NEXP * RANK] = np.asarray(L0_ffn_A).reshape(NEXP * RANK, KT, P).transpose(2, 1, 0)
    lora_router[:, :, NEXP * RANK:NEXP * RANK + NROUTE] = \
        np.asarray(L0_ffn_router_W).reshape(NROUTE, KT, P).transpose(2, 1, 0)
    fresh = np.ones((HG, NROUTE), np.float32)
    fresh[:, 0] = 0.0
    arrays = {
        "stream": np.stack(chunks), "xt": xt, "x": x, "decay": decay_tables(),
        "norm_w": np.asarray(L0_attn_norm_w).reshape(HEADS, P).T,
        "base_b": np.asarray(L0_ffn_base_b), "lora_router": lora_router, "router_b": np.asarray(L0_ffn_router_b),
        "expert_map": np.asarray(L0_ffn_expert_map),
        "ident_in": np.eye(P, dtype=np.float32), "ones_in": np.ones((P, 2), np.float32), "fresh_in": fresh.reshape(-1),
    }
    arrays = {n: np.ascontiguousarray(a) for n, a in arrays.items()}
    nc = bacc.Bacc("TRN2", target_bir_lowering=False, num_devices=1, dynamic_dma_scratch_size=1024)
    args = {n: nc.dram_tensor(n, a.shape, mybir.dt.from_np(a.dtype), kind="ExternalInput").ap()
            for n, a in arrays.items()}
    out = nc.dram_tensor("out", (TOK, HID), FP32, kind="ExternalOutput").ap()
    build(nc, out=out, **args)
    r = run_bass_kernel_spmd(nc, [arrays], core_ids=[0])
    return r.results[0]["out"].reshape(L0_attn_hidden_states.shape)
```
